# Optimizing a Trainium2 kernel written in Bass

```python
import numpy as np
import jax
import jax.numpy as jnp

def _softmax(x, axis=-1):
    return jax.nn.softmax(x, axis=axis)

def _gelu(x):
    return jax.nn.gelu(x, approximate=True)

def _silu(x):
    return jax.nn.silu(x)

def _sigmoid(x):
    return jax.nn.sigmoid(x)

def _layernorm(x, axis=-1, eps=1e-05):
    m = jnp.mean(x, axis=axis, keepdims=True)
    v = jnp.var(x, axis=axis, keepdims=True)
    return (x - m) / jnp.sqrt(v + eps)

def _scatter_add(tgt, idx, src, axis=0):
    return tgt.at[idx].add(src)

def _segment_sum(src, seg, n):
    return jax.ops.segment_sum(src, seg, n)
kernel_name = 'mk_xattn_ffn_d1_seqx_r2_4c7ecb'

def setup_inputs(seed: int=0):
    np.random.seed(seed)
    _w = jnp.asarray

    def _rec_inputs():
        import jax
        import jax.numpy as jnp
        _rk = jax.random.key(seed)
        x = 7.22e-05 + 1 * jax.random.normal(jax.random.fold_in(_rk, 1), (16, 512, 512), jnp.float32)
        _lenS = 512 - jax.random.randint(jax.random.fold_in(_rk, 7), (16,), 0, max(1, 512 // 4) + 1, jnp.int32)
        _lenS2 = 77 - jax.random.randint(jax.random.fold_in(_rk, 8), (16,), 0, max(1, 77 // 4) + 1, jnp.int32)
        _ctx_1024P = jax.random.normal(jax.random.fold_in(_rk, 11), (16, 16, 512), jnp.float32)
        _ctx_1024c = jax.random.dirichlet(jax.random.fold_in(_rk, 511), 0.3 * jnp.ones((16,), jnp.float32), (16, 77))
        _ctx_1024t = jnp.einsum('bsk,bkd->bsd', _ctx_1024c, _ctx_1024P)
        _ctx_1024t = _ctx_1024t * jax.lax.rsqrt(jnp.mean(jnp.square(_ctx_1024t)) + 1e-12) * 0.953939
        ctx_1024 = -0.000514642 + 1.00011 * (_ctx_1024t + 0.3 * jax.random.normal(jax.random.fold_in(_rk, 611), (16, 77, 512), jnp.float32))
        return (x, ctx_1024)
    x, ctx_1024 = _rec_inputs()

    def _L0_xattn_setup():
        import jax, jax.numpy as jnp
        import numpy as np
        B, L_ENC, L_DEC, D = (16, 256, 128, 512)
        key = jax.random.key(seed)
        k1, k2, k3, k4, k5, k6 = jax.random.split(key, 6)
        encoder_hc = jax.random.normal(k1, (B, L_ENC, D), dtype=jnp.float32)
        decoder_hq = jax.random.normal(k2, (B, L_DEC, D), dtype=jnp.float32)
        w_sim = jax.random.normal(k3, (3 * D,), dtype=jnp.float32) * 0.02
        b_sim = jax.random.normal(k4, (1,), dtype=jnp.float32) * 0.02
        W_qv = jax.random.normal(k5, (4 * D, D), dtype=jnp.float32) * 0.02
        b_qv = jax.random.normal(k6, (D,), dtype=jnp.float32) * 0.02
        return {'encoder_hc': encoder_hc, 'decoder_hq': decoder_hq, 'w_sim': w_sim, 'b_sim': b_sim, 'W_qv': W_qv, 'b_qv': b_qv}
    _L0_xattn_all = _L0_xattn_setup()
    _L0_xattn_in = {k: v for k, v in _L0_xattn_all.items() if k in ('w_sim', 'b_sim', 'W_qv', 'b_qv')}
    del _L0_xattn_all

    def _L0_ffn_setup():
        import jax, jax.numpy as jnp
        import numpy as np
        B, S, D_MODEL, D_FF = (4, 1024, 512, 2048)

        def _quantum_transform(hidden, theta, w_real, w_imag):
            imag = w_imag * jnp.sin(theta + hidden * 0.1)
            quantum_phase = jnp.cos(theta) * w_real + jnp.sin(theta) * w_imag
            return hidden + quantum_phase * imag * 0.1
        key = jax.random.key(seed)
        ks = jax.random.split(key, 8)
        return {'x': jax.random.normal(ks[0], (B, S, D_MODEL), dtype=jnp.float32), 'W1': jax.random.normal(ks[1], (D_MODEL, D_FF), dtype=jnp.float32) * (1.0 / np.sqrt(D_MODEL)), 'b1': jnp.zeros((D_FF,), dtype=jnp.float32), 'quantum_phases': jax.random.normal(ks[2], (D_FF,), dtype=jnp.float32) * (2.0 * np.pi), 'quantum_weights_real': jax.random.normal(ks[3], (D_FF,), dtype=jnp.float32) * 0.1, 'quantum_weights_imag': jax.random.normal(ks[4], (D_FF,), dtype=jnp.float32) * 0.1, 'W2': jax.random.normal(ks[5], (D_FF, D_MODEL), dtype=jnp.float32) * (1.0 / np.sqrt(D_FF)), 'b2': jnp.zeros((D_MODEL,), dtype=jnp.float32)}
    _L0_ffn_all = _L0_ffn_setup()
    _L0_ffn_in = {k: v for k, v in _L0_ffn_all.items() if k in ('W1', 'b1', 'quantum_phases', 'quantum_weights_real', 'quantum_weights_imag', 'W2', 'b2')}
    del _L0_ffn_all
    return {'x': x, 'ctx_1024': ctx_1024, 'L0_xattn_w_sim': _L0_xattn_in['w_sim'], 'L0_xattn_b_sim': _L0_xattn_in['b_sim'], 'L0_xattn_W_qv': _L0_xattn_in['W_qv'], 'L0_xattn_b_qv': _L0_xattn_in['b_qv'], 'L0_ffn_W1': _L0_ffn_in['W1'], 'L0_ffn_b1': _L0_ffn_in['b1'], 'L0_ffn_quantum_phases': _L0_ffn_in['quantum_phases'], 'L0_ffn_quantum_weights_real': _L0_ffn_in['quantum_weights_real'], 'L0_ffn_quantum_weights_imag': _L0_ffn_in['quantum_weights_imag'], 'L0_ffn_W2': _L0_ffn_in['W2'], 'L0_ffn_b2': _L0_ffn_in['b2']}

def reference(x, ctx_1024, L0_xattn_w_sim, L0_xattn_b_sim, L0_xattn_W_qv, L0_xattn_b_qv, L0_ffn_W1, L0_ffn_b1, L0_ffn_quantum_phases, L0_ffn_quantum_weights_real, L0_ffn_quantum_weights_imag, L0_ffn_W2, L0_ffn_b2):
    import jax
    import jax.numpy as jnp

    def _L0_xattn_ref(encoder_hc, decoder_hq, w_sim, b_sim, W_qv, b_qv):
        import jax, jax.numpy as jnp
        import numpy as np
        B, L_ENC, L_DEC, D = (16, 256, 128, 512)
        d = encoder_hc.shape[-1]
        w1, w2, w3 = (w_sim[:d], w_sim[d:2 * d], w_sim[2 * d:])
        Sim = (encoder_hc @ w1)[:, :, None] + (decoder_hq @ w2)[:, None, :] + jnp.einsum('bid,bjd->bij', encoder_hc * w3, decoder_hq) + b_sim[0]
        A = jax.nn.softmax(Sim, axis=2)
        hq_hat = jnp.einsum('bij,bjd->bid', A, decoder_hq)
        Batt = jax.nn.softmax(jnp.max(Sim, axis=2), axis=1)
        hc_bar = jnp.einsum('bi,bid->bd', Batt, encoder_hc)[:, None, :]
        hc_hat = jnp.broadcast_to(hc_bar, encoder_hc.shape)
        feats = jnp.concatenate([encoder_hc, hq_hat, encoder_hc * hq_hat, encoder_hc * hc_hat], axis=-1)
        hcq = feats @ W_qv + b_qv
        return hcq

    def _L0_ffn_ref(x, W1, b1, quantum_phases, quantum_weights_real, quantum_weights_imag, W2, b2):
        import jax, jax.numpy as jnp
        import numpy as np
        B, S, D_MODEL, D_FF = (4, 1024, 512, 2048)

        def _quantum_transform(hidden, theta, w_real, w_imag):
            imag = w_imag * jnp.sin(theta + hidden * 0.1)
            quantum_phase = jnp.cos(theta) * w_real + jnp.sin(theta) * w_imag
            return hidden + quantum_phase * imag * 0.1
        hidden = jnp.einsum('bsd,df->bsf', x, W1) + b1
        q = _quantum_transform(hidden, quantum_phases, quantum_weights_real, quantum_weights_imag)
        act = jax.nn.relu(q)
        return jnp.einsum('bsf,fd->bsd', act, W2) + b2
    x = x + _L0_xattn_ref(_layernorm(x, axis=-1), ctx_1024, L0_xattn_w_sim, L0_xattn_b_sim, L0_xattn_W_qv, L0_xattn_b_qv)
    x = x + _L0_ffn_ref(_layernorm(x, axis=-1), L0_ffn_W1, L0_ffn_b1, L0_ffn_quantum_phases, L0_ffn_quantum_weights_real, L0_ffn_quantum_weights_imag, L0_ffn_W2, L0_ffn_b2)
    return x

_drawn_inputs = setup_inputs


def setup_inputs(seed=0):
    import zlib

    import numpy as np

    out = dict(_drawn_inputs(seed))
    spreads = {'L0_ffn_b1': (0.0, 0.1), 'L0_ffn_b2': (0.0, 0.1)}
    factors = {'L0_xattn_b_qv': 3.124,
     'L0_ffn_quantum_phases': 8.0,
     'L0_ffn_quantum_weights_real': 41.652,
     'L0_ffn_quantum_weights_imag': 8.0}
    for name, (base, spread) in spreads.items():
        noise = np.random.default_rng([zlib.crc32(name.encode()), seed]).standard_normal(out[name].shape)
        drawn = base * np.exp(spread * noise) if base else spread * noise
        out[name] = jnp.asarray(drawn.astype(out[name].dtype))
    for name, factor in factors.items():
        out[name] = (out[name] * factor).astype(out[name].dtype)
    return out
```

```python
from contextlib import ExitStack

import numpy as np

import concourse.bass as bass
from concourse import mybir

ALU = mybir.AluOpType
ACT = mybir.ActivationFunctionType
AX = mybir.AxisListType
F32 = mybir.dt.float32
F32R = mybir.dt.float32r

P = 128
TWO_PI = 2 * np.pi
TURN = 1 / TWO_PI
TWO_PI_BELOW = float(np.nextafter(np.float32(TWO_PI), np.float32(0)))
PI_BELOW = float(np.nextafter(np.float32(np.pi), np.float32(0)))
ROUND = 1.5 * 2.0 ** 23
TP1 = 6.28125
TP2 = float(np.float32(np.round((TWO_PI - TP1) * 2 ** 20) / 2 ** 20))
TP3 = float(np.float32(TWO_PI - TP1 - TP2))
EPS = 1e-5


def xattn_ffn(nc, x, ctx_rows, w_sim, b_sim, W_qv, b_qv, W1, b1, theta, w_real, w_imag, W2, b2, out):
    B, R, D = x.shape
    J = ctx_rows.shape[1]
    F = W1.shape[1]
    C = D // P
    RT = R // P
    FT = F // P
    CR = 112
    CN = B * J // CR
    NV = 4 * FT + 2 * C
    LAG = 3
    NA = 9
    HSCALE = float(0.1 * TURN)
    assert R == 512 and D == 512 and CN * CR == B * J and FT % 4 == 0 and B % 2 == 0

    x_rows = x.rearrange("b (t p) d -> b p t d", p=P)
    out_rows = out.rearrange("b (t p) d -> b p t d", p=P)
    ctx_flat = ctx_rows.rearrange("b j d -> (b j) d")
    w1_dram = W1.rearrange("(c p) f -> p c f", p=P)
    w2_dram = W2.rearrange("(f p) d -> f p d", p=P)
    wqv_dram = W_qv.rearrange("(q c p) d -> q p c d", q=4, p=P)

    w2_split = nc.dram_tensor("w2_split", [FT, P, 2 * D], F32).ap()
    wq_split = nc.dram_tensor("wq_split", [C, P, 2 * D], F32).ap()
    hq_split = nc.dram_tensor("hq_split", [B * J, 2 * D], F32).ap()
    hqw_split = nc.dram_tensor("hqw_split", [B * J, 2 * D], F32).ap()
    g_split = nc.dram_tensor("g_split", [P, 2 * C, B * J], F32).ap()
    v_dram = nc.dram_tensor("v_dram", [B * J, 1], F32).ap()

    with ExitStack() as ctx:
        def sb(name, shape, dt=F32):
            return ctx.enter_context(nc.sbuf_tensor(name, shape, dt))

        def psum(name, shape):
            return ctx.enter_context(nc.psum_tensor(name, shape, F32))

        def sem(name):
            return ctx.enter_context(nc.semaphore(name))

        acc = psum("acc", [P, RT, D])
        hid = psum("hid", [P, 2, R])
        mis = psum("mis", [P, 2, 512])

        w1_sb = sb("w1_sb", [P, C, F])
        w1s = sb("w1s", [P, 2, 2, C, P], F32R)
        w2s = sb("w2s", [P, 4, 2, D], F32R)
        w0_sb = sb("w0_sb", [P, C, D])
        w3_sb = sb("w3_sb", [P, C, D])
        wqs = sb("wqs", [P, 2, 2, D], F32R)
        T = sb("T", [P, 2, 2, C, R], F32R)
        X = sb("X", [P, 2, RT, D])
        xin = sb("xin", [P, 2, D])
        h2 = sb("h2", [P, 2, R])
        ph = sb("ph", [P, 2, R])
        kk = sb("kk", [P, R])
        act = sb("act", [P, 4, 2, R], F32R)
        prs = sb("prs", [P, 2, 2, R], F32R)
        w0s = sb("w0s", [P, 2, 2, D], F32R)
        full = sb("full", [P, R])
        tmp_w = sb("tmp_w", [P, D])
        tmp_p = sb("tmp_p", [P, R])
        bqv_bc = sb("bqv_bc", [P, D])
        b2_bc = sb("b2_bc", [P, D])
        simt = sb("simt", [J, R])
        prob = sb("prob", [P, RT, J])
        at_s = sb("at_s", [J, 2, R], F32R)
        e_bc = sb("e_bc", [P, R])
        hqs = sb("hqs", [P, 2, D], F32R)
        hqw = sb("hqw", [P, 2, D], F32R)
        gs = sb("gs", [P, 2 * C, J], F32R)
        ident = sb("ident", [P, P])
        vj = sb("vj", [P, 1])
        cols = sb("cols", [P, NV])
        phase, wre, wim, b1c = (cols[:, k * FT:(k + 1) * FT] for k in range(4))
        w1c, w3c = (cols[:, 4 * FT + k * C:4 * FT + (k + 1) * C] for k in range(2))
        kth = sb("kth", [P, FT])
        arg = sb("arg", [P, 2, FT])
        trig = sb("trig", [P, 2, FT])
        hbias = sb("hbias", [P, FT])
        camp = sb("camp", [P, FT])
        bsim = sb("bsim", [P, 1])
        vraw = sb("vraw", [P, 1])
        st = sb("st", [P, RT, 6])
        mv = sb("mv", [P, RT, 3])
        dev = sb("dev", [P, RT])
        mscale = sb("mscale", [P, RT, 3])
        quarter = sb("quarter", [P, RT])
        vareps = sb("vareps", [P, RT])
        mhalf = sb("mhalf", [P, RT])
        eps_t = sb("eps_t", [P, RT])
        rstd = sb("rstd", [P, RT])
        rmax = sb("rmax", [P, RT])
        rsum = sb("rsum", [P, RT])
        rrec = sb("rrec", [P, RT])
        gmax = sb("gmax", [P, 1])
        esum = sb("esum", [P, 1])
        erec = sb("erec", [P, 1])
        hb_raw = sb("hb_raw", [P, C])
        hb = sb("hb", [P, C])

        s_const = sem("s_const"); s_w1 = sem("s_w1"); s_w03 = sem("s_w03"); s_ident0 = sem("s_ident0")
        s_ident = sem("s_ident"); s_chain = sem("s_chain"); s_args = sem("s_args"); s_trig = sem("s_trig")
        s_consts = sem("s_consts"); s_mhalf = sem("s_mhalf"); s_cols = sem("s_cols"); s_w1q_raw = sem("s_w1q_raw")
        s_w1q_hi = sem("s_w1q_hi"); s_w1q_lo = sem("s_w1q_lo")
        c_raw = sem("c_raw"); c_hqhi = sem("c_hqhi"); c_hqlo = sem("c_hqlo"); c_vr = sem("c_vr"); c_v = sem("c_v")
        c_stored = sem("c_stored"); c_tr = sem("c_tr"); c_thi = sem("c_thi"); c_tlo = sem("c_tlo")
        c_g = sem("c_g"); c_ghi = sem("c_ghi"); c_glo = sem("c_glo"); c_mm = sem("c_mm")
        c_whi = sem("c_whi"); c_wlo = sem("c_wlo")
        r_raw = [sem(f"r_raw{i}") for i in range(2)]; r_hi = sem("r_hi"); r_lo = sem("r_lo")
        r_stored = [sem(f"r_stored{i}") for i in range(2)]
        w1_hi = sem("w1_hi"); w1_lo = sem("w1_lo"); w2_in = [sem(f"w2_in{i}") for i in range(4)]
        hid_done = sem("hid_done"); t_done = sem("t_done"); h2_done = sem("h2_done"); k_done = sem("k_done")
        r_done = sem("r_done"); s_done = sem("s_done"); q_done = sem("q_done")
        act_hi = sem("act_hi"); act_lo = sem("act_lo"); ffn2_done = sem("ffn2_done")
        a_evac = sem("a_evac"); b_evac = sem("b_evac"); out_stored = sem("out_stored")
        ctx_in = sem("ctx_in"); xin_in = [sem(f"xin_in{i}") for i in range(2)]; x_in = sem("x_in")
        wq_in = [sem(f"wq_in{i}") for i in range(2)]
        st1 = sem("st1"); mo1 = sem("mo1"); rs1 = sem("rs1"); xn1 = sem("xn1"); tr1 = sem("tr1")
        t1_hi = sem("t1_hi"); t1_lo = sem("t1_lo"); sim_done = sem("sim_done"); simt_done = sem("simt_done")
        simr_done = sem("simr_done"); rmax_done = sem("rmax_done"); shift_done = sem("shift_done")
        exp_done = sem("exp_done"); rsum_done = sem("rsum_done"); rrec_done = sem("rrec_done")
        prob_done = sem("prob_done"); mbc_done = sem("mbc_done"); gmax_done = sem("gmax_done")
        ebc_done = sem("ebc_done"); erec_done = sem("erec_done"); at_done = sem("at_done")
        at_hi = sem("at_hi"); at_lo = sem("at_lo"); hqh_done = sem("hqh_done"); full_done = sem("full_done")
        hbr_done = sem("hbr_done"); hb_done = sem("hb_done")
        w0t_done = sem("w0t_done"); w0_hi = sem("w0_hi"); w0_lo = sem("w0_lo")
        prt_done = sem("prt_done"); pr_hi = sem("pr_hi"); pr_lo = sem("pr_lo")
        chunk_done = sem("chunk_done"); att_done = sem("att_done")
        xb_done = sem("xb_done"); x2_done = sem("x2_done"); xb2_done = sem("xb2_done")
        st2 = sem("st2"); mo2 = sem("mo2"); rs2 = sem("rs2"); xn2 = sem("xn2"); tr2 = sem("tr2")
        t2_hi = sem("t2_hi"); t2_lo = sem("t2_lo")

        def need(eng, s, count):
            if isinstance(count, int) and count <= 0:
                return
            eng.wait_ge(s, count)

        def settle(eng):
            eng.wait_ge(s_ident, 1)

        def batches(eng, attention_first, body, rest):
            attention_first()
            body(0, 0, True, False)
            with eng.Fori(0, (B - 2) // 2) as i:
                body(2 * i + 1, 1, False, False)
                body(2 * i + 2, 0, False, False)
            body(B - 1, (B - 1) % 2, False, True)
            rest()

        block = ctx.enter_context(nc.Block())

        @block.sync
        def _(sp):
            col = lambda v: v.rearrange("(t p) -> t p", p=P)
            at = lambda k, n: tmp_w[k:k + n, 0:P]
            row = lambda v, n: v.rearrange("(a d) -> a d", a=1).to_broadcast([n, D])
            sp.dma_start(X[:, 1], wqv_dram[1]).then_inc(s_w1q_raw, 16)
            consts = [(at(0, FT), col(theta)), (at(FT, FT), col(w_real)), (at(2 * FT, FT), col(w_imag)),
                      (at(3 * FT, FT), col(b1)), (at(4 * FT, C), col(w_sim[0:D])),
                      (at(4 * FT + C, C), col(w_sim[2 * D:3 * D])),
                      (bsim[:], b_sim.rearrange("(a d) -> a d", a=1).to_broadcast([P, 1])),
                      (e_bc[:], row(w_sim[D:2 * D], P)), (bqv_bc[:], row(b_qv, P)), (b2_bc[:], row(b2, P))]
            for dst, src in consts:
                sp.dma_start(dst, src).then_inc(s_const, 16)
            with sp.Fori(0, CN) as i:
                need(sp, c_hqlo, i)
                need(sp, c_vr, i)
                need(sp, c_tr, i)
                sp.dma_start(X[0:CR, 0, 0], ctx_flat[bass.ds(i * CR, CR), :]).then_inc(c_raw, 16)
                sp.wait_ge(c_hqlo, i + 1)
                sp.dma_start(hq_split[bass.ds(i * CR, CR), :],
                             hqs[0:CR].bitcast(F32).rearrange("p a d -> p (a d)")).then_inc(c_stored, 16)
                settle(sp)
                sp.wait_ge(c_v, i + 1)
                sp.dma_start(v_dram[bass.ds(i * CR, CR), :], vj[0:CR]).then_inc(c_stored, 16)
                sp.wait_ge(c_glo, i + 1)
                for a in range(2):
                    sp.dma_start(g_split[:, a * C:(a + 1) * C, bass.ds(i * CR, CR)],
                                 act[:, 1, a, 0:C * CR].bitcast(F32).rearrange("p (c j) -> p c j", c=C)
                                 ).then_inc(c_stored, 16)
                sp.wait_ge(c_wlo, i + 1)
                sp.dma_start(hqw_split[bass.ds(i * CR, CR), :],
                             hqw[0:CR].bitcast(F32).rearrange("p a d -> p (a d)")).then_inc(c_stored, 16)
            sp.dma_start(w0_sb[:], wqv_dram[0]).then_inc(s_w03, 16)
            sp.dma_start(w3_sb[:], wqv_dram[3]).then_inc(s_w03, 16)
            sp.dma_start(w1_sb[:], w1_dram).then_inc(s_w1, 16)
            def weight_in(k, src):
                need(sp, r_lo, k - 1)
                sp.dma_start(X[:, 0, 2 + k % 2], src).then_inc(r_raw[k % 2], 16)

            def weight_out(k, dst):
                sp.wait_ge(r_lo, k + 1)
                sp.dma_start(dst, w2s[:, k % 2].bitcast(F32).rearrange("p a d -> p (a d)")
                             ).then_inc(r_stored[k % 2], 16)
            for k in range(C + FT + 1):
                if k < C + FT:
                    weight_in(k, wqv_dram[2, :, k] if k < C else w2_dram[k - C])
                if k >= 1:
                    weight_out(k - 1, wq_split[k - 1] if k - 1 < C else w2_split[k - 1 - C])
            sp.wait_ge(c_stored, 16 * 5 * CN)
            for a in range(2):
                sp.wait_ge(r_stored[a], 16 * (C + FT) // 2)

            def w2_load(b, f):
                g = FT * b + f
                need(sp, ffn2_done, g - 3)
                sp.dma_start(w2s[:, f % 4].bitcast(F32).rearrange("p a d -> p (a d)"), w2_split[f]
                             ).then_inc(w2_in[f % 4], 16)

            def ctx_load(n):
                need(sp, att_done, RT * n)
                rows = bass.ds(n * J, J)
                sp.dma_start(gs[:].bitcast(F32), g_split[:, :, rows]).then_inc(ctx_in, 16)
                sp.dma_start(vj[0:J], v_dram[rows, :]).then_inc(ctx_in, 16)
                sp.dma_start(hqs[0:J].bitcast(F32).rearrange("p a d -> p (a d)"), hq_split[rows, :]
                             ).then_inc(ctx_in, 16)
                sp.dma_start(hqw[0:J].bitcast(F32).rearrange("p a d -> p (a d)"), hqw_split[rows, :]
                             ).then_inc(ctx_in, 16)

            def xin_load(n, t):
                if t < 2:
                    need(sp, tr2, RT * n - 2 + t + 1)
                else:
                    sp.wait_ge(tr1, RT * n + t - 1)
                sp.dma_start(xin[:, t % 2], x_rows[bass.ds(n, 1), :, t].rearrange("b p d -> (b p) d")
                             ).then_inc(xin_in[t % 2], 16)

            def x_load(n, par):
                need(sp, out_stored, 16 * (n - 1))
                sp.dma_start(X[:, par], x_rows[bass.ds(n, 1)].rearrange("b p t d -> (b p) t d")
                             ).then_inc(x_in, 16)

            def wq_load(n, c):
                if c < 2:
                    need(sp, att_done, RT * n)
                else:
                    sp.wait_ge(chunk_done, (C - 1) * n + c - 1)
                sp.dma_start(wqs[:, c % 2].bitcast(F32).rearrange("p a d -> p (a d)"), wq_split[c]
                             ).then_inc(wq_in[c % 2], 16)

            def store(b, par):
                sp.wait_ge(b_evac, RT * (b + 1))
                sp.dma_start(out_rows[bass.ds(b, 1)].rearrange("b p t d -> (b p) t d"), X[:, par]
                             ).then_inc(out_stored, 16)

            def attention_first():
                ctx_load(0)
                xin_load(0, 0)
                xin_load(0, 1)
                x_load(0, 0)
                xin_load(0, 2)
                xin_load(0, 3)
                for c in range(C):
                    wq_load(0, c)

            def body(b, par, first, last):
                n, pn = b + 1, 1 - par
                for f in range(FT):
                    w2_load(b, f)
                    if f == 3 and not first:
                        store(b - 1, pn)
                    if last:
                        continue
                    if f == 0:
                        xin_load(n, 0)
                        xin_load(n, 1)
                        ctx_load(n)
                    if f == 1:
                        xin_load(n, 2)
                        xin_load(n, 3)
                    if f == 5:
                        x_load(n, pn)
                    if f == NA - 2:
                        wq_load(n, 0)
                        wq_load(n, 1)
                    if f == NA:
                        wq_load(n, 2)
                        wq_load(n, 3)

            def rest():
                store(B - 1, (B - 1) % 2)
                sp.wait_ge(out_stored, 16 * B)

            batches(sp, attention_first, body, rest)

        @block.tensor
        def _(pe):
            def three(dst, w_hi, w_lo, m_hi, m_lo, start, stop, done=None):
                pe.matmul(dst, w_hi, m_hi, start=start, stop=False)
                pe.matmul(dst, w_hi, m_lo, start=False, stop=False)
                mm = pe.matmul(dst, w_lo, m_hi, start=False, stop=stop)
                if done is not None:
                    mm.then_inc(done, 1)

            pe.wait_ge(s_ident, 1)
            pe.wait_ge(s_const, 160)
            pe.transpose(hid[:, 0, 0:NV], tmp_w[0:NV, 0:P], ident[0:NV, 0:NV]).then_inc(s_cols, 1)
            pe.wait_ge(s_w1q_lo, C)
            with pe.Fori(0, CN) as i:
                pe.wait_ge(c_raw, 16 * i + 16)
                need(pe, c_tlo, i)
                need(pe, c_g, C * i)
                for c in range(C):
                    tr = pe.transpose(mis[:, 0, c * CR:(c + 1) * CR], X[0:CR, 0, 0, c * P:(c + 1) * P],
                                      ident[0:CR, 0:CR])
                tr.then_inc(c_tr, 1)
                pe.wait_ge(c_tlo, i + 1)
                need(pe, c_wlo, i)
                for c in range(C):
                    hq = act[:, 0, :, c * CR:(c + 1) * CR]
                    w = T[:, 0, :, c]
                    three(mis[0:CR, 1], hq[:, 0], hq[:, 1], w[:, 0], w[:, 1], c == 0, c == C - 1,
                          c_mm if c == C - 1 else None)

            def hidden(b, f, par):
                g = FT * b + f
                pe.wait_ge(w1_lo, g + 1)
                need(pe, h2_done, g - 1)
                if f == 0:
                    pe.wait_ge(t2_lo, RT * (b + 1))
                w = w1s[:, f % 2]
                for c in range(C):
                    three(hid[:, f % 2], w[:, 0, c], w[:, 1, c], T[:, par, 0, c], T[:, par, 1, c],
                          c == 0, c == C - 1, hid_done if c == C - 1 else None)

            def second(b, f, whole):
                g = FT * b + f
                pe.wait_ge(act_lo, g + 1)
                pe.wait_ge(w2_in[f % 4], 16 * (FT // 4 * b + f // 4 + 1))
                begins = f == 0 or (f == NA - 3 and not whole)
                ends = f == FT - 1 or (f == NA - 4 and not whole)
                for t in range(RT):
                    if f == 0:
                        need(pe, b_evac, RT * (b - 1) + t + 1)
                    if f == NA - 3 and not whole:
                        pe.wait_ge(x2_done, RT * (b + 1) + t + 1)
                    a = act[:, f % 4, :, t * P:(t + 1) * P]
                    three(acc[:, t], a[:, 0], a[:, 1], w2s[:, f % 4, 0], w2s[:, f % 4, 1], begins, ends,
                          ffn2_done if t == RT - 1 else None)

            def transpose_rows(n, t, ready, done, left):
                pe.wait_ge(ready, RT * n + t + 1)
                need(pe, *left)
                for c in range(C):
                    tr = pe.transpose(mis[:, t % 2, c * P:(c + 1) * P], xin[:, t % 2, c * P:(c + 1) * P], ident[:])
                tr.then_inc(done, 1)

            def tr_first(n, t):
                transpose_rows(n, t, xn1, tr1, (t2_lo, RT * n - 2 + t + 1) if t < 2 else (t1_lo, RT * n + t - 1))

            def tr_second(n, t):
                transpose_rows(n, t, xn2, tr2, (prt_done, C * n + 3 + t) if t < 2 else (t2_lo, RT * n + t - 1))

            def sim(n, par):
                pe.wait_ge(ctx_in, 64 * (n + 1))
                pe.wait_ge(t1_lo, RT * (n + 1))
                for c in range(C):
                    three(mis[0:J, 0], gs[:, c], gs[:, C + c], T[:, par, 0, c], T[:, par, 1, c],
                          c == 0, c == C - 1, sim_done if c == C - 1 else None)

            def sim_rows(n):
                pe.wait_ge(simt_done, n + 1)
                for t in range(RT):
                    tr = pe.transpose(mis[:, 1, t * J:(t + 1) * J], simt[:, t * P:(t + 1) * P], ident[0:J, 0:J])
                tr.then_inc(simr_done, 1)

            def spread_max(n):
                pe.wait_ge(rmax_done, n + 1)
                for t in range(RT):
                    tr = pe.transpose(mis[:, 0, t * P:(t + 1) * P], rmax[:, t:t + 1].to_broadcast([P, P]), ident[:])
                tr.then_inc(mbc_done, 1)

            def prob_turn(n):
                pe.wait_ge(prob_done, n + 1)
                for t in range(RT):
                    tr = pe.transpose(mis[0:J, 1, t * P:(t + 1) * P], prob[:, t], ident[:])
                tr.then_inc(at_done, 1)

            def hq_hat(n, c):
                if c == 0:
                    pe.wait_ge(at_lo, n + 1)
                    pe.wait_ge(ebc_done, n + 1)
                if c >= 2:
                    pe.wait_ge(prt_done, C * n + c - 1)
                hq = hqs[0:J, :, c * P:(c + 1) * P]
                three(mis[:, c % 2], hq[:, 0], hq[:, 1], at_s[:, 0], at_s[:, 1], True, True, hqh_done)

            def products(n, par, first):
                hq_hat(n, 1)
                for t in range(RT):
                    if not first:
                        pe.wait_ge(a_evac, RT * (n - 1) + t + 1)
                    a = at_s[:, :, t * P:(t + 1) * P]
                    three(acc[:, t], a[:, 0], a[:, 1], hqw[0:J, 0], hqw[0:J, 1], True, False)
                for c in range(C):
                    pe.wait_ge(w0_lo, C * n + c + 1)
                    for t in range(RT):
                        a = T[:, par, :, c, t * P:(t + 1) * P]
                        w = w0s[:, c % 2]
                        three(acc[:, t], a[:, 0], a[:, 1], w[:, 0], w[:, 1], False, False)
                        if c == C - 1:
                            product_tile(n, c, t)
                    if c < C - 1:
                        for t in range(RT):
                            product_tile(n, c, t)
                    if c + 2 < C:
                        hq_hat(n, c + 2)

            def product_tile(n, c, t):
                if t == 0:
                    pe.wait_ge(pr_lo, C * n + c + 1)
                    pe.wait_ge(wq_in[c % 2], 16 * (C // 2 * n + c // 2 + 1))
                a = prs[:, c % 2, :, t * P:(t + 1) * P]
                w = wqs[:, c % 2]
                three(acc[:, t], a[:, 0], a[:, 1], w[:, 0], w[:, 1], False, c == C - 1,
                      att_done if c == C - 1 else (chunk_done if t == RT - 1 else None))

            def attention_first():
                for t in range(RT):
                    tr_first(0, t)
                sim(0, 0)
                sim_rows(0)
                spread_max(0)
                prob_turn(0)
                hq_hat(0, 0)
                products(0, 0, True)
                for t in range(RT):
                    tr_second(0, t)

            def body(b, par, first, last):
                n, pn = b + 1, 1 - par
                for f in range(FT):
                    hidden(b, f, par)
                    if not last:
                        if f == 1:
                            tr_first(n, 0)
                            tr_first(n, 1)
                        if f == 3:
                            tr_first(n, 2)
                            tr_first(n, 3)
                        if f == 4:
                            sim(n, pn)
                        if f == 5:
                            sim_rows(n)
                        if f == 6:
                            spread_max(n)
                        if f == 7:
                            prob_turn(n)
                        if f == 8:
                            hq_hat(n, 0)
                        if f == NA:
                            products(n, pn, False)
                            continue
                        if f == NA + 1:
                            second(b, NA - LAG, False)
                        if f == NA + 4:
                            tr_second(n, 0)
                            tr_second(n, 1)
                        if f == NA + 5:
                            tr_second(n, 2)
                            tr_second(n, 3)
                    if f >= LAG:
                        second(b, f - LAG, last)
                    elif not first:
                        second(b - 1, FT + f - LAG, False)

            def rest():
                for f in range(FT - LAG, FT):
                    second(B - 1, f, True)

            batches(pe, attention_first, body, rest)

        @block.scalar
        def _(sc):
            for c in range(C):
                if c == 0:
                    sc.wait_ge(s_w1q_raw, 16)
                nc.scalar.copy(T[:, 0, 0, c], X[:, 1, c]).then_inc(s_w1q_hi, 1)
            sc.wait_ge(s_args, 1)
            nc.scalar.activation(trig[:], arg[:], ACT.Sin).then_inc(s_trig, 1)
            with sc.Fori(0, CN) as i:
                sc.wait_ge(c_raw, 16 * i + 16)
                need(sc, c_stored, 80 * i)
                nc.scalar.copy(hqs[0:CR, 0], X[0:CR, 0, 0]).then_inc(c_hqhi, 1)
                sc.wait_ge(c_tr, i + 1)
                need(sc, c_mm, i)
                nc.scalar.copy(act[:, 0, 0, 0:C * CR], mis[:, 0, 0:C * CR]).then_inc(c_thi, 1)
                sc.wait_ge(c_g, C * i + C)
                nc.scalar.copy(act[:, 1, 0, 0:C * CR], kk[:, 0:C * CR]).then_inc(c_ghi, 1)
                sc.wait_ge(c_mm, i + 1)
                nc.scalar.copy(hqw[0:CR, 0], mis[0:CR, 1]).then_inc(c_whi, 1)
            for k in range(C + FT):
                sc.wait_ge(r_raw[k % 2], 16 * (k // 2 + 1))
                need(sc, r_stored[k % 2], 16 * (k // 2))
                nc.scalar.copy(w2s[:, k % 2, 0], X[:, 0, 2 + k % 2]).then_inc(r_hi, 1)

            def w1_high(g, f, fresh):
                if not fresh:
                    sc.wait_ge(hid_done, g - 1)
                nc.scalar.copy(w1s[:, f % 2, 0], w1_sb[:, :, f * P:(f + 1) * P]).then_inc(w1_hi, 1)

            def phase_and_hidden(b, f):
                g = FT * b + f
                sc.wait_ge(hid_done, g + 1)
                need(sc, q_done, g - 1)
                nc.scalar.activation(ph[:, f % 2], hid[:, f % 2], ACT.Identity, bias=hbias[:, f:f + 1],
                                     scale=HSCALE).then_inc(t_done, 1)
                need(sc, act_lo, g - 1)
                nc.scalar.activation(h2[:, f % 2], hid[:, f % 2], ACT.Identity, bias=b1c[:, f:f + 1],
                                     scale=1.0).then_inc(h2_done, 1)

            def relu_high(g, f):
                sc.wait_ge(q_done, g + 1)
                need(sc, ffn2_done, g - 3)
                nc.scalar.activation(act[:, f % 4, 0], h2[:, f % 2], ACT.Relu).then_inc(act_hi, 1)

            def sine(b, f):
                sc.wait_ge(r_done, FT * b + f + 1)
                nc.scalar.activation(ph[:, f % 2], ph[:, f % 2], ACT.Sin, scale=TWO_PI_BELOW).then_inc(s_done, 1)

            def turned_high(n, t, par, ready, done):
                sc.wait_ge(ready, RT * n + t + 1)
                nc.scalar.copy(T[:, par, 0, :, t * P:(t + 1) * P],
                               mis[:, t % 2].rearrange("p (c r) -> p c r", c=C)).then_inc(done, 1)

            def sim_bias(n):
                sc.wait_ge(sim_done, n + 1)
                nc.scalar.activation(simt[:], mis[0:J, 0], ACT.Identity, bias=vj[0:J], scale=1.0
                                     ).then_inc(simt_done, 1)

            def exponentials(n):
                sc.wait_ge(shift_done, n + 1)
                nc.scalar.activation(prob[:], prob[:], ACT.Exp).then_inc(exp_done, 1)
                sc.wait_ge(gmax_done, n + 1)
                nc.scalar.activation(e_bc[:], mis[:, 0], ACT.Exp, bias=gmax[:], scale=1.0, accum_out=esum[:]
                                     ).then_inc(ebc_done, 1)

            def prob_high(n):
                sc.wait_ge(at_done, n + 1)
                nc.scalar.copy(at_s[:, 0], mis[0:J, 1]).then_inc(at_hi, 1)

            def w0_high(n, c):
                sc.wait_ge(w0t_done, C * n + c + 1)
                nc.scalar.copy(w0s[:, c % 2, 0], tmp_w[:]).then_inc(w0_hi, 1)

            def pr_high(n, c):
                sc.wait_ge(prt_done, C * n + c + 1)
                nc.scalar.copy(prs[:, c % 2, 0], tmp_p[:]).then_inc(pr_hi, 1)

            def attention_first():
                for t in range(RT):
                    turned_high(0, t, 0, tr1, t1_hi)
                sim_bias(0)
                exponentials(0)
                prob_high(0)
                for c in range(C):
                    w0_high(0, c)
                    pr_high(0, c)
                for t in range(RT):
                    turned_high(0, t, 0, tr2, t2_hi)
                sc.wait_ge(s_w1, 16)
                w1_high(0, 0, True)
                w1_high(1, 1, True)

            def body(b, par, first, last):
                n, pn = b + 1, 1 - par
                for f in range(FT):
                    g = FT * b + f
                    phase_and_hidden(b, f)
                    if f > 0 or not first:
                        relu_high(g - 1, (f - 1) % FT)
                    if f < FT - 2 or not last:
                        w1_high(g + 2, (f + 2) % FT, False)
                    sine(b, f)
                    if last:
                        continue
                    if f == 1:
                        turned_high(n, 0, pn, tr1, t1_hi)
                        turned_high(n, 1, pn, tr1, t1_hi)
                    if f == 3:
                        turned_high(n, 2, pn, tr1, t1_hi)
                        turned_high(n, 3, pn, tr1, t1_hi)
                    if f == 4:
                        sim_bias(n)
                    if f == 6:
                        exponentials(n)
                    if f == 7:
                        prob_high(n)
                    if f == 8:
                        w0_high(n, 0)
                        pr_high(n, 0)
                    if f == NA:
                        for c in range(1, C):
                            w0_high(n, c)
                            pr_high(n, c)
                    if f == NA + 4:
                        turned_high(n, 0, pn, tr2, t2_hi)
                        turned_high(n, 1, pn, tr2, t2_hi)
                    if f == NA + 5:
                        turned_high(n, 2, pn, tr2, t2_hi)
                        turned_high(n, 3, pn, tr2, t2_hi)

            def rest():
                relu_high(FT * B - 1, FT - 1)

            batches(sc, attention_first, body, rest)

        @block.vector
        def _(ve):
            chain = [0]

            def link(ins):
                chain[0] += 1
                ins.then_inc(s_chain, 1)
                ve.wait_ge(s_chain, chain[0])

            def low(dst, value, high):
                return ve.tensor_tensor(dst, value, high.bitcast(F32), ALU.subtract)

            ve.wait_ge(s_cols, 1)
            link(ve.tensor_copy(cols[:], hid[:, 0, 0:NV]))
            link(ve.tensor_scalar(kth[:], phase[:], float(TURN), ROUND, ALU.mult, ALU.add))
            link(ve.tensor_scalar(kth[:], kth[:], -ROUND, None, ALU.add))
            for part in (TP1, TP2, TP3):
                link(ve.scalar_tensor_tensor(out=phase[:], in0=kth[:], scalar=-part, in1=phase[:],
                                             op0=ALU.mult, op1=ALU.add))
            link(ve.tensor_scalar(arg[:, 0], phase[:], PI_BELOW, -PI_BELOW, ALU.min, ALU.max))
            link(ve.scalar_tensor_tensor(out=arg[:, 1], in0=arg[:, 0], scalar=-1.0, in1=arg[:, 0],
                                         op0=ALU.mult, op1=ALU.max))
            link(ve.tensor_scalar(arg[:, 1], arg[:, 1], -1.0, float(np.pi / 2), ALU.mult, ALU.add))
            ve.tensor_scalar(kth[:], b1c[:], HSCALE, None, ALU.mult).then_inc(s_args, 1)
            ve.wait_ge(s_args, 1)
            link(ve.scalar_tensor_tensor(out=hbias[:], in0=phase[:], scalar=float(TURN), in1=kth[:],
                                         op0=ALU.mult, op1=ALU.add))
            ve.wait_ge(s_trig, 1)
            link(ve.tensor_tensor(camp[:], trig[:, 1], wre[:], ALU.mult))
            link(ve.tensor_tensor(kth[:], trig[:, 0], wim[:], ALU.mult))
            link(ve.tensor_tensor(camp[:], camp[:], kth[:], ALU.add))
            link(ve.scalar_tensor_tensor(out=camp[:], in0=camp[:], scalar=0.1, in1=wim[:],
                                         op0=ALU.mult, op1=ALU.mult))
            for c in range(C):
                ve.wait_ge(s_w1q_hi, c + 1)
                low(T[:, 0, 1, c], X[:, 1, c], T[:, 0, 0, c]).then_inc(s_w1q_lo, 1)
            with ve.Fori(0, CN) as i:
                ve.wait_ge(c_raw, 16 * i + 16)
                need(ve, c_stored, 80 * i)
                ve.tensor_tensor_reduce(out=tmp_w[0:CR], in0=X[0:CR, 0, 0], in1=e_bc[0:CR], scale=1.0, scalar=0.0,
                                        op0=ALU.mult, op1=ALU.add, accum_out=vraw[0:CR]).then_inc(c_vr, 1)
                ve.wait_ge(c_hqhi, i + 1)
                low(hqs[0:CR, 1], X[0:CR, 0, 0], hqs[0:CR, 0]).then_inc(c_hqlo, 1)
                ve.wait_ge(c_vr, i + 1)
                ve.tensor_tensor(vj[0:CR], vraw[0:CR], bsim[0:CR], ALU.add).then_inc(c_v, 1)
                ve.wait_ge(c_thi, i + 1)
                low(act[:, 0, 1, 0:C * CR], mis[:, 0, 0:C * CR], act[:, 0, 0, 0:C * CR]).then_inc(c_tlo, 1)
                for c in range(C):
                    ve.tensor_scalar(kk[:, c * CR:(c + 1) * CR], mis[:, 0, c * CR:(c + 1) * CR], w3c[:, c:c + 1],
                                     w1c[:, c:c + 1], ALU.mult, ALU.add).then_inc(c_g, 1)
                ve.wait_ge(c_ghi, i + 1)
                low(act[:, 1, 1, 0:C * CR], kk[:, 0:C * CR], act[:, 1, 0, 0:C * CR]).then_inc(c_glo, 1)
                ve.wait_ge(c_whi, i + 1)
                low(hqw[0:CR, 1], mis[0:CR, 1], hqw[0:CR, 0]).then_inc(c_wlo, 1)
            ve.wait_ge(s_w03, 32)

            def sine_term(g, f):
                ve.wait_ge(s_done, g + 1)
                ve.scalar_tensor_tensor(out=h2[:, f % 2], in0=ph[:, f % 2], scalar=camp[:, f:f + 1],
                                        in1=h2[:, f % 2], op0=ALU.mult, op1=ALU.add).then_inc(q_done, 1)

            def reduce_phase(b, f):
                g = FT * b + f
                ve.wait_ge(t_done, g + 1)
                need(ve, r_done, g)
                ve.tensor_scalar(kk[:], ph[:, f % 2], ROUND, -ROUND, ALU.add, ALU.add).then_inc(k_done, 1)
                ve.wait_ge(k_done, g + 1)
                ve.tensor_tensor(ph[:, f % 2], ph[:, f % 2], kk[:], ALU.subtract).then_inc(r_done, 1)

            def relu_low(g, f):
                ve.wait_ge(act_hi, g + 1)
                ve.scalar_tensor_tensor(out=act[:, f % 4, 1], in0=h2[:, f % 2], scalar=0.0,
                                        in1=act[:, f % 4, 0].bitcast(F32), op0=ALU.max, op1=ALU.subtract
                                        ).then_inc(act_lo, 1)

            def stats_first(n, t):
                ve.wait_ge(xin_in[t % 2], 16 * (RT // 2 * n + t // 2 + 1))
                ve.bn_stats(st[:, t], xin[:, t % 2]).then_inc(st1, 1)

            def norm_first(n, t):
                ve.wait_ge(rs1, RT // 2 * n + t // 2 + 1)
                ve.tensor_scalar(xin[:, t % 2], xin[:, t % 2], mv[:, t, 1:2], rstd[:, t:t + 1],
                                 ALU.subtract, ALU.mult).then_inc(xn1, 1)

            def turned_low(n, t, par, high_done, done):
                ve.wait_ge(high_done, RT * n + t + 1)
                low(T[:, par, 1, :, t * P:(t + 1) * P], mis[:, t % 2].rearrange("p (c r) -> p c r", c=C),
                    T[:, par, 0, :, t * P:(t + 1) * P]).then_inc(done, 1)

            def row_max(n):
                ve.wait_ge(simr_done, n + 1)
                s = mis[:, 1, 0:RT * J].rearrange("p (t j) -> p t j", t=RT)
                ve.tensor_reduce(rmax[:], s, AX.X, ALU.max).then_inc(rmax_done, 1)
                ve.wait_ge(rmax_done, n + 1)
                ve.tensor_tensor(prob[:], s, rmax[:].unsqueeze(2).to_broadcast([P, RT, J]), ALU.subtract
                                 ).then_inc(shift_done, 1)

            def probabilities(n):
                ve.wait_ge(mbc_done, n + 1)
                ve.tensor_reduce(gmax[:], mis[:, 0], AX.X, ALU.max, negate=True).then_inc(gmax_done, 1)
                ve.wait_ge(exp_done, n + 1)
                ve.tensor_reduce(rsum[:], prob[:], AX.X, ALU.add).then_inc(rsum_done, 1)
                ve.wait_ge(rsum_done, n + 1)
                ve.reciprocal(rrec[:], rsum[:]).then_inc(rrec_done, 1)
                ve.wait_ge(rrec_done, n + 1)
                ve.tensor_tensor(prob[:], prob[:], rrec[:].unsqueeze(2).to_broadcast([P, RT, J]), ALU.mult
                                 ).then_inc(prob_done, 1)
                ve.wait_ge(ebc_done, n + 1)
                ve.reciprocal(erec[:], esum[:]).then_inc(erec_done, 1)

            def prob_low(n):
                ve.wait_ge(at_hi, n + 1)
                low(at_s[:, 1], mis[0:J, 1], at_s[:, 0]).then_inc(at_lo, 1)

            def row_mean(n):
                for c in range(C):
                    ve.wait_ge(full_done, 2 * C * n + c + 1)
                    need(ve, pr_lo if c == 0 else hbr_done, C * n + c)
                    ve.tensor_tensor_reduce(out=tmp_p[:], in0=full[:], in1=e_bc[:], scale=1.0, scalar=0.0,
                                            op0=ALU.mult, op1=ALU.add, accum_out=hb_raw[:, c:c + 1]
                                            ).then_inc(hbr_done, 1)
                ve.wait_ge(hbr_done, C * (n + 1))
                ve.wait_ge(erec_done, n + 1)
                ve.tensor_scalar(hb[:], hb_raw[:], erec[:], None, ALU.mult).then_inc(hb_done, 1)

            def w0_chunk(n, c):
                if c == 0:
                    ve.wait_ge(hb_done, n + 1)
                need(ve, w0_lo, C * n + c)
                ve.scalar_tensor_tensor(out=tmp_w[:], in0=w3_sb[:, c], scalar=hb[:, c:c + 1], in1=w0_sb[:, c],
                                        op0=ALU.mult, op1=ALU.add).then_inc(w0t_done, 1)

            def w0_low(n, c):
                ve.wait_ge(w0_hi, C * n + c + 1)
                low(w0s[:, c % 2, 1], tmp_w[:], w0s[:, c % 2, 0]).then_inc(w0_lo, 1)

            def pr_chunk(n, c):
                ve.wait_ge(hqh_done, C * n + c + 1)
                ve.wait_ge(full_done, 2 * C * n + C + c + 1)
                if c >= 2:
                    ve.wait_ge(chunk_done, (C - 1) * n + c - 1)
                if c == 0:
                    ve.wait_ge(hbr_done, C * (n + 1))
                else:
                    ve.wait_ge(pr_lo, C * n + c)
                ve.tensor_tensor(tmp_p[:], mis[:, c % 2], full[:], ALU.mult).then_inc(prt_done, 1)

            def pr_low_(n, c):
                ve.wait_ge(pr_hi, C * n + c + 1)
                low(prs[:, c % 2, 1], tmp_p[:], prs[:, c % 2, 0]).then_inc(pr_lo, 1)

            def chunk(n, c):
                if c >= 2:
                    ve.wait_ge(chunk_done, (C - 1) * n + c - 1)
                w0_chunk(n, c)
                pr_chunk(n, c)
                w0_low(n, c)
                pr_low_(n, c)

            def evacuate(par, t, done):
                ve.tensor_tensor(X[:, par, t], X[:, par, t], acc[:, t], ALU.add).then_inc(done, 1)

            def add_attention(n, par):
                ve.wait_ge(xb_done, n + 1)
                for t in range(RT):
                    ve.wait_ge(att_done, RT * n + t + 1)
                    evacuate(par, t, x2_done)

            def stats_second(n, par):
                for t in range(RT):
                    ve.wait_ge(x2_done, RT * n + t + 1)
                    ve.bn_stats(st[:, t], X[:, par, t]).then_inc(st2, 1)

            def norm_second(n, par, t):
                ve.wait_ge(rs2, n + 1)
                if t >= 2:
                    ve.wait_ge(tr2, RT * n + t - 1)
                ve.tensor_scalar(xin[:, t % 2], X[:, par, t], mv[:, t, 1:2], rstd[:, t:t + 1],
                                 ALU.subtract, ALU.mult).then_inc(xn2, 1)

            def add_first_part(b, par):
                ve.wait_ge(xb2_done, b + 1)
                ve.wait_ge(ffn2_done, FT * b + NA - LAG)
                for t in range(RT):
                    evacuate(par, t, a_evac)

            def add_last_part(b, par, whole):
                ve.wait_ge(ffn2_done, FT * (b + 1))
                if whole:
                    ve.wait_ge(xb2_done, b + 1)
                else:
                    ve.wait_ge(a_evac, RT * (b + 1))
                for t in range(RT):
                    evacuate(par, t, b_evac)

            def attention_first():
                for t in range(RT):
                    stats_first(0, t)
                    if t % 2 == 1:
                        norm_first(0, t - 1)
                        norm_first(0, t)
                for t in range(RT):
                    turned_low(0, t, 0, t1_hi, t1_lo)
                row_max(0)
                probabilities(0)
                prob_low(0)
                row_mean(0)
                for c in range(C):
                    chunk(0, c)
                add_attention(0, 0)
                stats_second(0, 0)
                for t in range(RT):
                    norm_second(0, 0, t)
                    if t >= 1:
                        turned_low(0, t - 1, 0, t2_hi, t2_lo)
                turned_low(0, RT - 1, 0, t2_hi, t2_lo)

            def body(b, par, first, last):
                n, pn = b + 1, 1 - par
                for f in range(FT):
                    g = FT * b + f
                    if f == NA and not last:
                        add_first_part(b, par)
                    reduce_phase(b, f)
                    if f > 0 or not first:
                        sine_term(g - 1, (f - 1) % FT)
                        relu_low(g - 1, (f - 1) % FT)
                    if f == 3 and not first:
                        add_last_part(b - 1, pn, False)
                    if last:
                        continue
                    if f == 0:
                        stats_first(n, 0)
                        stats_first(n, 1)
                        norm_first(n, 0)
                        norm_first(n, 1)
                    if f == 1:
                        turned_low(n, 0, pn, t1_hi, t1_lo)
                        turned_low(n, 1, pn, t1_hi, t1_lo)
                    if f == 2:
                        stats_first(n, 2)
                        stats_first(n, 3)
                        norm_first(n, 2)
                        norm_first(n, 3)
                    if f == 3:
                        turned_low(n, 2, pn, t1_hi, t1_lo)
                        turned_low(n, 3, pn, t1_hi, t1_lo)
                    if f == 5:
                        row_max(n)
                    if f == 6:
                        probabilities(n)
                    if f == 7:
                        prob_low(n)
                        row_mean(n)
                    if f == 8:
                        chunk(n, 0)
                    if f == NA:
                        for c in range(1, C):
                            chunk(n, c)
                        add_attention(n, pn)
                    if f == NA + 1:
                        stats_second(n, pn)
                    if f == NA + 3:
                        norm_second(n, pn, 0)
                        norm_second(n, pn, 1)
                    if f == NA + 4:
                        turned_low(n, 0, pn, t2_hi, t2_lo)
                        turned_low(n, 1, pn, t2_hi, t2_lo)
                        norm_second(n, pn, 2)
                        norm_second(n, pn, 3)
                    if f == NA + 5:
                        turned_low(n, 2, pn, t2_hi, t2_lo)
                        turned_low(n, 3, pn, t2_hi, t2_lo)

            def rest():
                g = FT * B - 1
                sine_term(g, FT - 1)
                relu_low(g, FT - 1)
                add_last_part(B - 1, (B - 1) % 2, True)

            batches(ve, attention_first, body, rest)

        @block.gpsimd
        def _(po):
            po.memset(ident[:], 0.0).then_inc(s_ident0, 1)
            po.memset(mhalf[:], -0.5).then_inc(s_mhalf, 1)
            po.memset(eps_t[:], EPS).then_inc(s_mhalf, 1)
            po.memset(quarter[:], 0.25).then_inc(s_mhalf, 1)
            po.memset(mscale[:, :, 0:2], 0.5).then_inc(s_mhalf, 1)
            po.memset(mscale[:, :, 2:3], 1.0 / D).then_inc(s_mhalf, 1)
            po.wait_ge(s_ident0, 1)
            po.affine_select(out=ident[:], in_=ident[:], compare_op=ALU.not_equal, fill=1.0, base=0,
                             pattern=[[-1, P]], channel_multiplier=1).then_inc(s_ident, 1)
            for k in range(C + FT):
                po.wait_ge(r_hi, k + 1)
                po.tensor_tensor(w2s[:, k % 2, 1], X[:, 0, 2 + k % 2], w2s[:, k % 2, 0].bitcast(F32), ALU.subtract
                                 ).then_inc(r_lo, 1)
            po.wait_ge(s_mhalf, 5)

            def w1_low(g, f):
                po.wait_ge(w1_hi, g + 1)
                po.tensor_tensor(w1s[:, f % 2, 1], w1_sb[:, :, f * P:(f + 1) * P], w1s[:, f % 2, 0].bitcast(F32),
                                 ALU.subtract).then_inc(w1_lo, 1)

            def moments(t0, t1, stats_done, stats_count, step, count, done):
                po.wait_ge(stats_done, stats_count)
                halves = st[:, t0:t1].rearrange("p t (h k) -> p t h k", h=2)
                po.tensor_tensor(mv[:, t0:t1], halves[:, :, 0], halves[:, :, 1], ALU.add).then_inc(step, 1)
                po.tensor_tensor(dev[:, t0:t1], halves[:, :, 0, 1], halves[:, :, 1, 1], ALU.subtract).then_inc(step, 1)
                po.wait_ge(step, count - 3)
                po.tensor_tensor(mv[:, t0:t1], mv[:, t0:t1], mscale[:, t0:t1], ALU.mult).then_inc(step, 1)
                po.tensor_tensor(dev[:, t0:t1], dev[:, t0:t1], dev[:, t0:t1], ALU.mult).then_inc(step, 1)
                po.wait_ge(step, count - 1)
                po.tensor_tensor(dev[:, t0:t1], dev[:, t0:t1], quarter[:, t0:t1], ALU.mult).then_inc(step, 1)
                po.wait_ge(step, count)
                po.tensor_tensor(vareps[:, t0:t1], mv[:, t0:t1, 2], dev[:, t0:t1], ALU.add).then_inc(step, 1)
                po.wait_ge(step, count + 1)
                po.tensor_tensor(vareps[:, t0:t1], vareps[:, t0:t1], eps_t[:, t0:t1], ALU.add).then_inc(step, 1)
                po.wait_ge(step, count + 2)
                po.tensor_tensor(rstd[:, t0:t1], vareps[:, t0:t1], mhalf[:, t0:t1], ALU.pow).then_inc(done, 1)

            def deviation_first(n, half):
                moments(2 * half, 2 * half + 2, st1, RT * n + 2 * half + 2, mo1, 7 * (2 * n + half) + 5, rs1)

            def deviation_second(n):
                moments(0, RT, st2, RT * (n + 1), mo2, 7 * n + 5, rs2)

            def whole(n, k, c, par):
                if k == 0:
                    need(po, prt_done, C * n)
                    po.wait_ge(t1_lo, RT * (n + 1))
                elif k <= C:
                    po.wait_ge(hbr_done, C * n + k)
                else:
                    po.wait_ge(prt_done, C * n + k - C)
                po.tensor_tensor(full[:], T[:, par, 0, c].bitcast(F32), T[:, par, 1, c].bitcast(F32), ALU.add
                                 ).then_inc(full_done, 1)

            def add_bqv(n, par):
                po.wait_ge(x_in, 16 * (n + 1))
                po.tensor_tensor(X[:, par], X[:, par], bqv_bc[:].unsqueeze(1).to_broadcast([P, RT, D]), ALU.add
                                 ).then_inc(xb_done, 1)

            def add_b2(n, par):
                po.wait_ge(xn2, RT * (n + 1))
                po.tensor_tensor(X[:, par], X[:, par], b2_bc[:].unsqueeze(1).to_broadcast([P, RT, D]), ALU.add
                                 ).then_inc(xb2_done, 1)

            def attention_first():
                po.wait_ge(s_const, 160)
                deviation_first(0, 0)
                deviation_first(0, 1)
                for k in range(2 * C):
                    whole(0, k, k % C, 0)
                    if k == C:
                        add_bqv(0, 0)
                deviation_second(0)
                add_b2(0, 0)
                po.wait_ge(s_w1, 16)
                w1_low(0, 0)
                w1_low(1, 1)

            def body(b, par, first, last):
                n, pn = b + 1, 1 - par
                for f in range(FT):
                    g = FT * b + f
                    if f < FT - 2 or not last:
                        w1_low(g + 2, (f + 2) % FT)
                    if last:
                        continue
                    if f == 0:
                        deviation_first(n, 0)
                    if f == 2:
                        deviation_first(n, 1)
                    if f == 6:
                        whole(n, 0, 0, pn)
                    if f == 7:
                        for k in range(1, C):
                            whole(n, k, k, pn)
                    if f == 8:
                        whole(n, C, 0, pn)
                        add_bqv(n, pn)
                    if f == NA:
                        for k in range(C + 1, 2 * C):
                            whole(n, k, k - C, pn)
                    if f == NA + 1:
                        deviation_second(n)
                    if f == NA + 4:
                        add_b2(n, pn)

            batches(po, attention_first, body, lambda: None)


_INS = ['x', 'ctx_1024', 'L0_xattn_w_sim', 'L0_xattn_b_sim', 'L0_xattn_W_qv', 'L0_xattn_b_qv', 'L0_ffn_W1', 'L0_ffn_b1',
        'L0_ffn_quantum_phases', 'L0_ffn_quantum_weights_real', 'L0_ffn_quantum_weights_imag', 'L0_ffn_W2', 'L0_ffn_b2']


def kernel(**inputs):
    import numpy as _np
    import concourse.bacc as _bacc
    from concourse import mybir as _mybir
    from concourse.bass_utils import run_bass_kernel_spmd as _run

    nc = _bacc.Bacc("TRN2", target_bir_lowering=False, num_devices=1)
    arrays, args = {}, []
    for name in _INS:
        a = _np.ascontiguousarray(inputs[name])
        arrays[f"in_{name}"] = a
        args.append(nc.dram_tensor(f"in_{name}", a.shape, _mybir.dt.from_np(a.dtype), kind="ExternalInput").ap())
    shape = inputs['x'].shape
    args.append(nc.dram_tensor("out_x", shape, _mybir.dt.float32, kind="ExternalOutput").ap())
    xattn_ffn(nc, *args)
    r = _run(nc, [arrays], core_ids=[0])
    return r.results[0]["out_x"]
```

```python
from contextlib import ExitStack

import numpy as np

import concourse.bass as bass
from concourse import mybir

ALU = mybir.AluOpType
ACT = mybir.ActivationFunctionType
AX = mybir.AxisListType
F32 = mybir.dt.float32
F32R = mybir.dt.float32r

P = 128
TWO_PI = 2 * np.pi
TURN = 1 / TWO_PI
TWO_PI_BELOW = float(np.nextafter(np.float32(TWO_PI), np.float32(0)))
PI_BELOW = float(np.nextafter(np.float32(np.pi), np.float32(0)))
ROUND = 1.5 * 2.0 ** 23
TP1 = 6.28125
TP2 = float(np.float32(np.round((TWO_PI - TP1) * 2 ** 20) / 2 ** 20))
TP3 = float(np.float32(TWO_PI - TP1 - TP2))
EPS = 1e-5


def xattn_ffn(nc, x, ctx_rows, w_sim, b_sim, W_qv, b_qv, W1, b1, theta, w_real, w_imag, W2, b2, out):
    B, R, D = x.shape
    J = ctx_rows.shape[1]
    F = W1.shape[1]
    C = D // P
    RT = R // P
    FT = F // P
    CR = 112
    CN = B * J // CR
    NV = 4 * FT + 2 * C
    LAG = 3
    NA = 10
    HSCALE = float(0.1 * TURN)
    assert R == 512 and D == 512 and CN * CR == B * J and FT % 4 == 0 and B % 2 == 0

    x_rows = x.rearrange("b (t p) d -> b p t d", p=P)
    out_rows = out.rearrange("b (t p) d -> b p t d", p=P)
    ctx_flat = ctx_rows.rearrange("b j d -> (b j) d")
    w1_dram = W1.rearrange("(c p) f -> p c f", p=P)
    w2_dram = W2.rearrange("(f p) d -> f p d", p=P)
    wqv_dram = W_qv.rearrange("(q c p) d -> q p c d", q=4, p=P)

    w2_split = nc.dram_tensor("w2_split", [FT, P, 2 * D], F32).ap()
    wq_split = nc.dram_tensor("wq_split", [C, P, 2 * D], F32).ap()
    hq_split = nc.dram_tensor("hq_split", [B * J, 2 * D], F32).ap()
    hqw_split = nc.dram_tensor("hqw_split", [B * J, 2 * D], F32).ap()
    g_split = nc.dram_tensor("g_split", [P, 2 * C, B * J], F32).ap()
    v_dram = nc.dram_tensor("v_dram", [B * J, 1], F32).ap()

    with ExitStack() as ctx:
        def sb(name, shape, dt=F32):
            return ctx.enter_context(nc.sbuf_tensor(name, shape, dt))

        def psum(name, shape):
            return ctx.enter_context(nc.psum_tensor(name, shape, F32))

        def sem(name):
            return ctx.enter_context(nc.semaphore(name))

        acc = psum("acc", [P, RT, D])
        hid = psum("hid", [P, 2, R])
        mis = psum("mis", [P, 2, 512])

        w1_sb = sb("w1_sb", [P, C, F])
        w1s = sb("w1s", [P, 2, 2, C, P], F32R)
        w2s = sb("w2s", [P, 4, 2, D], F32R)
        w0_sb = sb("w0_sb", [P, C, D])
        w3_sb = sb("w3_sb", [P, C, D])
        wqs = sb("wqs", [P, 2, 2, D], F32R)
        T = sb("T", [P, 2, 2, C, R], F32R)
        X = sb("X", [P, 2, RT, D])
        xin = sb("xin", [P, 2, D])
        h2 = sb("h2", [P, 2, R])
        ph = sb("ph", [P, 2, R])
        kk = sb("kk", [P, R])
        act = sb("act", [P, 4, 2, R], F32R)
        prs = sb("prs", [P, 2, 2, R], F32R)
        w0s = sb("w0s", [P, 2, 2, D], F32R)
        full = sb("full", [P, C, R])
        tmp_w = sb("tmp_w", [P, D])
        bqv_bc = sb("bqv_bc", [P, D])
        b2_bc = sb("b2_bc", [P, D])
        simt = tmp_w[0:J]
        prob = sb("prob", [P, RT, J])
        at_s = sb("at_s", [J, 2, R], F32R)
        e_bc = sb("e_bc", [P, R])
        hqs = sb("hqs", [P, 2, D], F32R)
        hqw = sb("hqw", [P, 2, D], F32R)
        gs = sb("gs", [P, 2 * C, J], F32R)
        ident = sb("ident", [P, P])
        vj = sb("vj", [P, 1])
        vsum = sb("vsum", [P, 2])
        cols = sb("cols", [P, NV])
        phase, wre, wim, b1c = (cols[:, k * FT:(k + 1) * FT] for k in range(4))
        w1c, w3c = (cols[:, 4 * FT + k * C:4 * FT + (k + 1) * C] for k in range(2))
        kth = sb("kth", [P, FT])
        arg = sb("arg", [P, 2, FT])
        trig = sb("trig", [P, 2, FT])
        hbias = sb("hbias", [P, FT])
        camp = sb("camp", [P, FT])
        bsim = sb("bsim", [P, 1])
        vraw = sb("vraw", [P, 2])
        st = sb("st", [P, RT, 6])
        mv = sb("mv", [P, RT, 3])
        dev = sb("dev", [P, RT])
        mscale = sb("mscale", [P, RT, 3])
        quarter = sb("quarter", [P, RT])
        ones = sb("ones", [P, 1])
        vareps = sb("vareps", [P, RT])
        mhalf = sb("mhalf", [P, RT])
        eps_t = sb("eps_t", [P, RT])
        rstd = sb("rstd", [P, RT])
        rmax = sb("rmax", [P, RT])
        rsum = sb("rsum", [P, RT])
        rrec = sb("rrec", [P, RT])
        gmax = sb("gmax", [P, 1])
        esum = sb("esum", [P, 1])
        erec = sb("erec", [P, 1])
        hb_raw = sb("hb_raw", [P, C])
        hb = sb("hb", [P, C])

        s_const = sem("s_const"); s_w1 = sem("s_w1"); s_w03 = sem("s_w03"); s_ident0 = sem("s_ident0")
        s_ident = sem("s_ident"); s_chain = sem("s_chain"); s_args = sem("s_args"); s_trig = sem("s_trig")
        s_consts = sem("s_consts"); s_mhalf = sem("s_mhalf"); s_cols = sem("s_cols"); s_w1q_raw = sem("s_w1q_raw")
        s_w1q_hi = sem("s_w1q_hi"); s_w1q_lo = sem("s_w1q_lo")
        c_raw = [sem(f"c_raw{i}") for i in range(2)]; c_hqhi = sem("c_hqhi"); c_hqlo = sem("c_hqlo"); c_vr = sem("c_vr"); c_v = sem("c_v")
        c_stored = [sem(f"c_stored{i}") for i in range(2)]; c_tr = sem("c_tr"); c_thi = sem("c_thi"); c_tlo = sem("c_tlo")
        c_g = sem("c_g"); c_ghi = sem("c_ghi"); c_glo = sem("c_glo"); c_mm = sem("c_mm")
        c_whi = sem("c_whi"); c_wlo = sem("c_wlo")
        r_raw = [sem(f"r_raw{i}") for i in range(2)]; r_hi = sem("r_hi"); r_lo = sem("r_lo")
        r_stored = [sem(f"r_stored{i}") for i in range(2)]
        w1_hi = sem("w1_hi"); w1_lo = sem("w1_lo"); w2_in = [sem(f"w2_in{i}") for i in range(4)]
        hid_done = sem("hid_done"); t_done = sem("t_done"); h2_done = sem("h2_done"); k_done = sem("k_done")
        r_done = sem("r_done"); s_done = sem("s_done"); q_done = sem("q_done")
        act_hi = sem("act_hi"); act_lo = sem("act_lo"); ffn2_done = sem("ffn2_done")
        a_evac = sem("a_evac"); b_evac = sem("b_evac"); out_stored = sem("out_stored")
        ctx_in = sem("ctx_in"); xin_in = [sem(f"xin_in{i}") for i in range(2)]; x_in = sem("x_in")
        wq_in = [sem(f"wq_in{i}") for i in range(2)]
        st1 = sem("st1"); mo1 = sem("mo1"); rs1 = sem("rs1"); xn1 = sem("xn1"); tr1 = sem("tr1")
        t1_hi = sem("t1_hi"); t1_lo = sem("t1_lo"); sim_done = sem("sim_done"); simt_done = sem("simt_done")
        simr_done = sem("simr_done"); rmax_done = sem("rmax_done"); shift_done = sem("shift_done")
        exp_done = sem("exp_done"); rsum_done = sem("rsum_done"); rrec_done = sem("rrec_done")
        prob_done = sem("prob_done"); mbc_done = sem("mbc_done"); gmax_done = sem("gmax_done")
        ebc_done = sem("ebc_done"); erec_done = sem("erec_done"); at_done = sem("at_done")
        at_hi = sem("at_hi"); at_lo = sem("at_lo"); hqh_done = sem("hqh_done"); full_done = sem("full_done")
        hbr_done = sem("hbr_done"); hb_done = sem("hb_done")
        w0t_done = sem("w0t_done"); w0_hi = sem("w0_hi"); w0_lo = sem("w0_lo")
        prt_done = sem("prt_done"); pr_hi = sem("pr_hi"); pr_lo = sem("pr_lo")
        chunk_done = sem("chunk_done"); att_done = sem("att_done")
        xb_done = sem("xb_done"); x2_done = sem("x2_done"); xb2_done = sem("xb2_done")
        st2 = sem("st2"); mo2 = sem("mo2"); rs2 = sem("rs2"); xn2 = sem("xn2"); tr2 = sem("tr2")
        t2_hi = sem("t2_hi"); t2_lo = sem("t2_lo")

        def need(eng, s, count):
            if isinstance(count, int) and count <= 0:
                return
            eng.wait_ge(s, count)

        def settle(eng):
            eng.wait_ge(s_ident, 1)

        def batches(eng, attention_first, body, rest):
            attention_first()
            body(0, 0, True, False)
            with eng.Fori(0, (B - 2) // 2) as i:
                body(2 * i + 1, 1, False, False)
                body(2 * i + 2, 0, False, False)
            body(B - 1, (B - 1) % 2, False, True)
            rest()

        def context_steps(eng, step):
            step(0, 0, 0, False)
            step(1, 0, 1, False)
            with eng.Fori(1, CN // 2) as i:
                step(2 * i, i, 0, False)
                step(2 * i + 1, i, 1, False)
            step(CN - 1, CN // 2, 0, True)

        c_rows = [w0_sb[0:CR, q] for q in range(2)]
        c_split = [prs[0:CR, q] for q in range(2)]
        c_turned = [act[:, 2 * q, :, 0:C * CR] for q in range(2)]
        c_gfull = [ph[:, q, 0:C * CR] for q in range(2)]
        c_gsplit = [act[:, 2 * q + 1, :, 0:C * CR] for q in range(2)]
        c_product = [w0s[0:CR, q] for q in range(2)]
        w1q_raw, w1q = w3_sb, T[:, 1]
        w_raw = [X[:, 1, q] for q in range(2)]
        LATE = [(True, c) for c in range(C)] + [(False, f) for f in range(CN, FT)]

        block = ctx.enter_context(nc.Block())

        @block.sync
        def _(sp):
            col = lambda v: v.rearrange("(t p) -> t p", p=P)
            at = lambda k, n: tmp_w[k:k + n, 0:P]
            row = lambda v, n: v.rearrange("(a d) -> a d", a=1).to_broadcast([n, D])
            def xin_load(n, t):
                if t < 2:
                    need(sp, tr2, RT * n - 2 + t + 1)
                else:
                    sp.wait_ge(tr1, RT * n + t - 1)
                sp.dma_start(xin[:, t % 2], x_rows[bass.ds(n, 1), :, t].rearrange("b p d -> (b p) d")
                             ).then_inc(xin_in[t % 2], 16)

            xin_load(0, 0)
            xin_load(0, 1)
            sp.dma_start(w1q_raw[:], wqv_dram[1]).then_inc(s_w1q_raw, 16)
            consts = [(at(0, FT), col(theta)), (at(FT, FT), col(w_real)), (at(2 * FT, FT), col(w_imag)),
                      (at(3 * FT, FT), col(b1)), (at(4 * FT, C), col(w_sim[0:D])),
                      (at(4 * FT + C, C), col(w_sim[2 * D:3 * D])),
                      (bsim[:], b_sim.rearrange("(a d) -> a d", a=1).to_broadcast([P, 1])),
                      (e_bc[:], row(w_sim[D:2 * D], P)), (bqv_bc[:], row(b_qv, P)), (b2_bc[:], row(b2, P))]
            for dst, src in consts:
                sp.dma_start(dst, src).then_inc(s_const, 16)
            def rows_in(s, q):
                if not (isinstance(s, int) and s < 2):
                    need(sp, c_hqlo, s - 1)
                    need(sp, c_vr, s - 1)
                    need(sp, c_tr, s - 1)
                sp.dma_start(c_rows[q], ctx_flat[bass.ds(s * CR, CR), :]).then_inc(c_raw[q], 16)

            def rows_step(s, i, q, last):
                if not last:
                    rows_in(s + 1, 1 - q)
                    weight_in(s + 1, 1 - q, w2_dram[bass.ds(s + 1, 1)].rearrange("f p d -> (f p) d"))
                rows = bass.ds(s * CR, CR)
                sp.wait_ge(c_hqlo, s + 1)
                sp.dma_start(hq_split[rows, :], c_split[q].bitcast(F32).rearrange("p a d -> p (a d)")
                             ).then_inc(c_stored[q], 16)
                settle(sp)
                sp.wait_ge(c_v, s + 1)
                sp.dma_start(v_dram[rows, :], vsum[0:CR, q:q + 1]).then_inc(c_stored[q], 16)
                sp.wait_ge(c_glo, s + 1)
                for a in range(2):
                    sp.dma_start(g_split[:, a * C:(a + 1) * C, rows],
                                 c_gsplit[q][:, a].bitcast(F32).rearrange("p (c j) -> p c j", c=C)
                                 ).then_inc(c_stored[q], 16)
                sp.wait_ge(c_wlo, s + 1)
                sp.dma_start(hqw_split[rows, :], c_product[q].bitcast(F32).rearrange("p a d -> p (a d)")
                             ).then_inc(c_stored[q], 16)
                weight_out(s, q, w2_split[bass.ds(s, 1)].rearrange("f p d -> (f p) d"))
                if isinstance(s, int) and s == 1:
                    sp.wait_ge(c_stored[0], 16 * 5)
                    ctx_load(0)

            def ctx_load(n):
                need(sp, att_done, RT * n)
                rows = bass.ds(n * J, J)
                sp.dma_start(gs[:].bitcast(F32), g_split[:, :, rows]).then_inc(ctx_in, 16)
                sp.dma_start(vj[0:J], v_dram[rows, :]).then_inc(ctx_in, 16)
                sp.dma_start(hqs[0:J].bitcast(F32).rearrange("p a d -> p (a d)"), hq_split[rows, :]
                             ).then_inc(ctx_in, 16)
                sp.dma_start(hqw[0:J].bitcast(F32).rearrange("p a d -> p (a d)"), hqw_split[rows, :]
                             ).then_inc(ctx_in, 16)

            def weight_in(k, q, src):
                need(sp, r_lo, k - 1)
                sp.dma_start(w_raw[q], src).then_inc(r_raw[q], 16)

            def weight_out(k, q, dst):
                sp.wait_ge(r_lo, k + 1)
                sp.dma_start(dst, w2s[:, q].bitcast(F32).rearrange("p a d -> p (a d)")).then_inc(r_stored[q], 16)

            rows_in(0, 0)
            weight_in(0, 0, w2_dram[0])
            xin_load(0, 2)
            xin_load(0, 3)
            context_steps(sp, rows_step)
            sp.wait_ge(c_hqlo, CN)
            sp.wait_ge(c_vr, CN)
            sp.wait_ge(c_tr, CN)
            sp.wait_ge(s_w1q_lo, C)
            sp.dma_start(w0_sb[:], wqv_dram[0]).then_inc(s_w03, 16)
            sp.dma_start(w3_sb[:], wqv_dram[3]).then_inc(s_w03, 16)

            def w2_load(b, f):
                g = FT * b + f
                need(sp, ffn2_done, g - 3)
                sp.dma_start(w2s[:, f % 4].bitcast(F32).rearrange("p a d -> p (a d)"), w2_split[f]
                             ).then_inc(w2_in[f % 4], 16)

            def x_load(n, par):
                need(sp, out_stored, 16 * (n - 1))
                sp.dma_start(X[:, par], x_rows[bass.ds(n, 1)].rearrange("b p t d -> (b p) t d")
                             ).then_inc(x_in, 16)

            def wq_load(n, c):
                if c < 2:
                    need(sp, att_done, RT * n)
                else:
                    sp.wait_ge(chunk_done, (C - 1) * n + c - 1)
                sp.dma_start(wqs[:, c % 2].bitcast(F32).rearrange("p a d -> p (a d)"), wq_split[c]
                             ).then_inc(wq_in[c % 2], 16)

            def store(b, par):
                sp.wait_ge(b_evac, RT * (b + 1))
                sp.dma_start(out_rows[bass.ds(b, 1)].rearrange("b p t d -> (b p) t d"), X[:, par]
                             ).then_inc(out_stored, 16)

            def attention_first():
                def late_in(k):
                    is_q, c = LATE[k]
                    weight_in(CN + k, (CN + k) % 2, wqv_dram[2, :, c] if is_q else w2_dram[c])

                late_in(0)
                late_in(1)
                x_load(0, 0)
                for k in range(len(LATE)):
                    is_q, c = LATE[k]
                    weight_out(CN + k, (CN + k) % 2, wq_split[c] if is_q else w2_split[c])
                    if k + 2 < len(LATE):
                        late_in(k + 2)
                    if k == C - 1:
                        sp.dma_start(w1_sb[:], w1_dram).then_inc(s_w1, 16)
                    if k == C:
                        for q in range(2):
                            sp.wait_ge(r_stored[q], 16 * ((CN + C + 1 - q) // 2))
                        wq_load(0, 0)
                        wq_load(0, 1)
                for q in range(2):
                    sp.wait_ge(r_stored[q], 16 * ((CN + len(LATE) + 1 - q) // 2))
                    sp.wait_ge(c_stored[q], 16 * 5 * ((CN + 1 - q) // 2))
                wq_load(0, 2)
                wq_load(0, 3)

            def body(b, par, first, last):
                n, pn = b + 1, 1 - par
                for f in range(FT):
                    if f == 0 and not last:
                        xin_load(n, 0)
                        xin_load(n, 1)
                    w2_load(b, f)
                    if f == 0 and not last:
                        ctx_load(n)
                    if f == 3 and not first:
                        store(b - 1, pn)
                    if last:
                        continue
                    if f == 1:
                        xin_load(n, 2)
                        xin_load(n, 3)
                    if f == 5:
                        x_load(n, pn)
                    if f == NA - 2:
                        wq_load(n, 0)
                        wq_load(n, 1)
                    if f == NA:
                        wq_load(n, 2)
                        wq_load(n, 3)

            def rest():
                for t in range(RT):
                    sp.wait_ge(b_evac, RT * (B - 1) + t + 1)
                    sp.dma_start(out_rows[B - 1, :, t], X[:, (B - 1) % 2, t]).then_inc(out_stored, 16)
                sp.wait_ge(out_stored, 16 * (B - 1 + RT))

            batches(sp, attention_first, body, rest)

        @block.tensor
        def _(pe):
            def three(dst, w_hi, w_lo, m_hi, m_lo, start, stop, done=None):
                pe.matmul(dst, w_hi, m_hi, start=start, stop=False)
                pe.matmul(dst, w_hi, m_lo, start=False, stop=False)
                mm = pe.matmul(dst, w_lo, m_hi, start=False, stop=stop)
                if done is not None:
                    mm.then_inc(done, 1)

            pe.wait_ge(s_ident, 1)
            pe.wait_ge(s_const, 160)
            pe.transpose(hid[:, 0, 0:NV], tmp_w[0:NV, 0:P], ident[0:NV, 0:NV]).then_inc(s_cols, 1)
            def turn(s, i, q):
                pe.wait_ge(c_raw[q], 16 * i + 16)
                if not (isinstance(s, int) and s < 2):
                    pe.wait_ge(c_tlo, s - 1)
                    pe.wait_ge(c_g, C * (s - 1))
                for c in range(C):
                    tr = pe.transpose(mis[:, q, c * CR:(c + 1) * CR], c_rows[q][:, c * P:(c + 1) * P],
                                      ident[0:CR, 0:CR])
                tr.then_inc(c_tr, 1)

            def turn_and_multiply(s, i, q, last):
                if not last:
                    turn(s + 1, i + q, 1 - q)
                pe.wait_ge(c_tlo, s + 1)
                if not (isinstance(s, int) and s < 2):
                    pe.wait_ge(c_wlo, s - 1)
                for c in range(C):
                    hq = c_turned[q][:, :, c * CR:(c + 1) * CR]
                    w = w1q[:, :, c]
                    three(hid[0:CR, q], hq[:, 0], hq[:, 1], w[:, 0], w[:, 1], c == 0, c == C - 1,
                          c_mm if c == C - 1 else None)

            def hidden(b, f, par):
                g = FT * b + f
                pe.wait_ge(w1_lo, g + 1)
                need(pe, h2_done, g - 1)
                if f == 0:
                    pe.wait_ge(t2_lo, RT * (b + 1))
                w = w1s[:, f % 2]
                for c in range(C):
                    three(hid[:, f % 2], w[:, 0, c], w[:, 1, c], T[:, par, 0, c], T[:, par, 1, c],
                          c == 0, c == C - 1, hid_done if c == C - 1 else None)

            def second(b, f, whole):
                g = FT * b + f
                pe.wait_ge(act_lo, g + 1)
                pe.wait_ge(w2_in[f % 4], 16 * (FT // 4 * b + f // 4 + 1))
                begins = f == 0 or (f == NA - 3 and not whole)
                ends = f == FT - 1 or (f == NA - 4 and not whole)
                for t in range(RT):
                    if f == 0:
                        need(pe, b_evac, RT * (b - 1) + t + 1)
                    if f == NA - 3 and not whole:
                        pe.wait_ge(x2_done, RT * (b + 1) + t + 1)
                    a = act[:, f % 4, :, t * P:(t + 1) * P]
                    three(acc[:, t], a[:, 0], a[:, 1], w2s[:, f % 4, 0], w2s[:, f % 4, 1], begins, ends,
                          ffn2_done if t == RT - 1 else None)

            def transpose_rows(n, t, ready, done, left):
                pe.wait_ge(ready, RT * n + t + 1)
                need(pe, *left)
                for c in range(C):
                    tr = pe.transpose(mis[:, t % 2, c * P:(c + 1) * P], xin[:, t % 2, c * P:(c + 1) * P], ident[:])
                tr.then_inc(done, 1)

            def tr_first(n, t):
                transpose_rows(n, t, xn1, tr1, (t2_lo, RT * n - 2 + t + 1) if t < 2 else (t1_lo, RT * n + t - 1))

            def tr_second(n, t):
                transpose_rows(n, t, xn2, tr2, (prt_done, C * n + 3 + t) if t < 2 else (t2_lo, RT * n + t - 1))

            def sim(n, par):
                pe.wait_ge(ctx_in, 64 * (n + 1))
                pe.wait_ge(t1_lo, RT * (n + 1))
                for c in range(C):
                    three(mis[0:J, 0], gs[:, c], gs[:, C + c], T[:, par, 0, c], T[:, par, 1, c],
                          c == 0, c == C - 1, sim_done if c == C - 1 else None)

            def sim_rows(n):
                pe.wait_ge(simt_done, n + 1)
                for t in range(RT):
                    tr = pe.transpose(mis[:, 1, t * J:(t + 1) * J], simt[:, t * P:(t + 1) * P], ident[0:J, 0:J])
                tr.then_inc(simr_done, 1)

            def spread_max(n):
                pe.wait_ge(rmax_done, n + 1)
                for t in range(RT):
                    tr = pe.transpose(mis[:, 0, t * P:(t + 1) * P], rmax[:, t:t + 1].to_broadcast([P, P]), ident[:])
                tr.then_inc(mbc_done, 1)

            def prob_turn(n):
                pe.wait_ge(prob_done, n + 1)
                for t in range(RT):
                    tr = pe.transpose(mis[0:J, 1, t * P:(t + 1) * P], prob[:, t], ident[:])
                tr.then_inc(at_done, 1)

            def hq_hat(n, c):
                if c == 0:
                    pe.wait_ge(at_lo, n + 1)
                    pe.wait_ge(ebc_done, n + 1)
                if c >= 2:
                    pe.wait_ge(prt_done, C * n + c - 1)
                hq = hqs[0:J, :, c * P:(c + 1) * P]
                three(mis[:, c % 2], hq[:, 0], hq[:, 1], at_s[:, 0], at_s[:, 1], True, True, hqh_done)

            def products(n, par, first):
                hq_hat(n, 1)
                for t in range(RT):
                    if not first:
                        pe.wait_ge(a_evac, RT * (n - 1) + t + 1)
                    a = at_s[:, :, t * P:(t + 1) * P]
                    three(acc[:, t], a[:, 0], a[:, 1], hqw[0:J, 0], hqw[0:J, 1], True, False)
                for c in range(C):
                    pe.wait_ge(w0_lo, C * n + c + 1)
                    for t in range(RT):
                        a = T[:, par, :, c, t * P:(t + 1) * P]
                        w = w0s[:, c % 2]
                        three(acc[:, t], a[:, 0], a[:, 1], w[:, 0], w[:, 1], False, False)
                        if c == C - 1:
                            product_tile(n, c, t)
                    if c < C - 1:
                        for t in range(RT):
                            product_tile(n, c, t)
                    if c + 2 < C:
                        hq_hat(n, c + 2)

            def product_tile(n, c, t):
                if t == 0:
                    pe.wait_ge(pr_lo, C * n + c + 1)
                    pe.wait_ge(wq_in[c % 2], 16 * (C // 2 * n + c // 2 + 1))
                a = prs[:, c % 2, :, t * P:(t + 1) * P]
                w = wqs[:, c % 2]
                three(acc[:, t], a[:, 0], a[:, 1], w[:, 0], w[:, 1], False, c == C - 1,
                      att_done if c == C - 1 else (chunk_done if t == RT - 1 else None))

            for t in range(RT):
                tr_first(0, t)
            pe.wait_ge(s_w1q_lo, C)
            pe.wait_ge(t1_lo, RT)
            turn(0, 0, 0)
            context_steps(pe, turn_and_multiply)

            def attention_first():
                pe.wait_ge(c_g, C * CN)
                sim(0, 0)
                sim_rows(0)
                spread_max(0)
                prob_turn(0)
                hq_hat(0, 0)
                products(0, 0, True)
                for t in range(RT):
                    tr_second(0, t)

            def body(b, par, first, last):
                n, pn = b + 1, 1 - par
                for f in range(FT):
                    if f != NA + 1 or last:
                        hidden(b, f, par)
                    if f == 1 and not last:
                        tr_first(n, 0)
                        tr_first(n, 1)
                    if f == 6 and not last:
                        spread_max(n)
                    if f == NA - 1 and not last:
                        hq_hat(n, 0)
                    if f == NA and not last:
                        hidden(b, f + 1, par)
                        products(n, pn, False)
                        continue
                    if f == NA + 1 and not last:
                        continue
                    if f == NA + 2 and not last:
                        second(b, NA - LAG, False)
                        second(b, NA - LAG + 1, False)
                    if f >= LAG:
                        second(b, f - LAG, last)
                    elif not first:
                        second(b - 1, FT + f - LAG, False)
                    if last:
                        continue
                    if f == 3:
                        tr_first(n, 2)
                        tr_first(n, 3)
                    if f == 4:
                        sim(n, pn)
                    if f == 5:
                        sim_rows(n)
                    if f == 7:
                        prob_turn(n)
                    if f == NA + 3:
                        tr_second(n, 0)
                        tr_second(n, 1)
                    if f == NA + 4:
                        tr_second(n, 2)
                        tr_second(n, 3)

            def rest():
                for f in range(FT - LAG, FT):
                    second(B - 1, f, True)

            batches(pe, attention_first, body, rest)

        @block.scalar
        def _(sc):
            def turned_high(n, t, par, ready, done):
                sc.wait_ge(ready, RT * n + t + 1)
                nc.scalar.copy(T[:, par, 0, :, t * P:(t + 1) * P],
                               mis[:, t % 2].rearrange("p (c r) -> p c r", c=C)).then_inc(done, 1)

            for c in range(C):
                if c == 0:
                    sc.wait_ge(s_w1q_raw, 16)
                nc.scalar.copy(w1q[:, 0, c], w1q_raw[:, c]).then_inc(s_w1q_hi, 1)
            sc.wait_ge(s_args, 1)
            nc.scalar.activation(trig[:], arg[:], ACT.Sin).then_inc(s_trig, 1)
            for t in range(RT):
                turned_high(0, t, 0, tr1, t1_hi)

            def high_parts(s, i, q, last):
                sc.wait_ge(c_raw[q], 16 * i + 16)
                need(sc, c_stored[q], 80 * i)
                nc.scalar.copy(c_split[q][:, 0], c_rows[q]).then_inc(c_hqhi, 1)
                sc.wait_ge(c_tr, s + 1)
                need(sc, c_mm, s - 1)
                nc.scalar.copy(c_turned[q][:, 0], mis[:, q, 0:C * CR]).then_inc(c_thi, 1)
                need(sc, c_glo, s - 1)
                for c in range(2):
                    nc.scalar.activation(c_gfull[q][:, c * CR:(c + 1) * CR], mis[:, q, c * CR:(c + 1) * CR],
                                         ACT.Identity, bias=w1c[:, c:c + 1], scale=w3c[:, c:c + 1]
                                         ).then_inc(c_g, 1)
                sc.wait_ge(c_g, C * s + C)
                nc.scalar.copy(c_gsplit[q][:, 0], c_gfull[q]).then_inc(c_ghi, 1)
                sc.wait_ge(c_mm, s + 1)
                nc.scalar.copy(c_product[q][:, 0], hid[0:CR, q]).then_inc(c_whi, 1)

            context_steps(sc, high_parts)

            def w1_high(g, f, fresh):
                if not fresh:
                    sc.wait_ge(hid_done, g - 1)
                nc.scalar.copy(w1s[:, f % 2, 0], w1_sb[:, :, f * P:(f + 1) * P]).then_inc(w1_hi, 1)

            def phase_and_hidden(b, f):
                g = FT * b + f
                sc.wait_ge(hid_done, g + 1)
                need(sc, q_done, g - 1)
                nc.scalar.activation(ph[:, f % 2], hid[:, f % 2], ACT.Identity, bias=hbias[:, f:f + 1],
                                     scale=HSCALE).then_inc(t_done, 1)
                need(sc, act_lo, g - 1)
                nc.scalar.activation(h2[:, f % 2], hid[:, f % 2], ACT.Identity, bias=b1c[:, f:f + 1],
                                     scale=1.0).then_inc(h2_done, 1)

            def relu_high(g, f):
                sc.wait_ge(q_done, g + 1)
                need(sc, ffn2_done, g - 3)
                nc.scalar.activation(act[:, f % 4, 0], h2[:, f % 2], ACT.Relu).then_inc(act_hi, 1)

            def sine(b, f):
                sc.wait_ge(r_done, FT * b + f + 1)
                nc.scalar.activation(ph[:, f % 2], ph[:, f % 2], ACT.Sin, scale=TWO_PI_BELOW).then_inc(s_done, 1)

            def sim_bias(n):
                sc.wait_ge(sim_done, n + 1)
                nc.scalar.activation(simt[:], mis[0:J, 0], ACT.Identity, bias=vj[0:J], scale=1.0
                                     ).then_inc(simt_done, 1)

            def exponentials(n):
                sc.wait_ge(shift_done, n + 1)
                nc.scalar.activation(prob[:], prob[:], ACT.Exp).then_inc(exp_done, 1)
                sc.wait_ge(gmax_done, n + 1)
                nc.scalar.activation(e_bc[:], mis[:, 0], ACT.Exp, bias=gmax[:], scale=1.0, accum_out=esum[:]
                                     ).then_inc(ebc_done, 1)

            def prob_high(n):
                sc.wait_ge(at_done, n + 1)
                nc.scalar.copy(at_s[:, 0], mis[0:J, 1]).then_inc(at_hi, 1)

            def w0_high(n, c):
                sc.wait_ge(w0t_done, C * n + c + 1)
                nc.scalar.copy(w0s[:, c % 2, 0], tmp_w[:]).then_inc(w0_hi, 1)

            def pr_high(n, c):
                sc.wait_ge(prt_done, C * n + c + 1)
                nc.scalar.copy(prs[:, c % 2, 0], full[:, c]).then_inc(pr_hi, 1)

            def attention_first():
                sim_bias(0)
                exponentials(0)
                prob_high(0)
                for c in range(C):
                    w0_high(0, c)
                    pr_high(0, c)
                sc.wait_ge(s_w1, 16)
                w1_high(0, 0, True)
                w1_high(1, 1, True)
                for t in range(RT):
                    turned_high(0, t, 0, tr2, t2_hi)

            def body(b, par, first, last):
                n, pn = b + 1, 1 - par
                for f in range(FT):
                    g = FT * b + f
                    phase_and_hidden(b, f)
                    if f > 0 or not first:
                        relu_high(g - 1, (f - 1) % FT)
                    if f < FT - 2 or not last:
                        w1_high(g + 2, (f + 2) % FT, False)
                    sine(b, f)
                    if last:
                        continue
                    if f == 1:
                        turned_high(n, 0, pn, tr1, t1_hi)
                        turned_high(n, 1, pn, tr1, t1_hi)
                    if f == 3:
                        turned_high(n, 2, pn, tr1, t1_hi)
                        turned_high(n, 3, pn, tr1, t1_hi)
                    if f == 4:
                        sim_bias(n)
                    if f == 6:
                        exponentials(n)
                    if f == 7:
                        prob_high(n)
                    if f == NA - 1:
                        w0_high(n, 0)
                        pr_high(n, 0)
                    if f == NA:
                        for c in range(1, C):
                            w0_high(n, c)
                            pr_high(n, c)
                    if f == NA + 3:
                        turned_high(n, 0, pn, tr2, t2_hi)
                        turned_high(n, 1, pn, tr2, t2_hi)
                    if f == NA + 4:
                        turned_high(n, 2, pn, tr2, t2_hi)
                        turned_high(n, 3, pn, tr2, t2_hi)

            def rest():
                relu_high(FT * B - 1, FT - 1)

            batches(sc, attention_first, body, rest)

        @block.vector
        def _(ve):
            chain = [0]

            def link(ins):
                chain[0] += 1
                ins.then_inc(s_chain, 1)
                ve.wait_ge(s_chain, chain[0])

            def low(dst, value, high):
                return ve.tensor_tensor(dst, value, high.bitcast(F32), ALU.subtract)

            def stats_first(n, t):
                ve.wait_ge(xin_in[t % 2], 16 * (RT // 2 * n + t // 2 + 1))
                ve.bn_stats(st[:, t], xin[:, t % 2]).then_inc(st1, 1)

            def norm_first(n, t):
                ve.wait_ge(rs1, RT // 2 * n + t // 2 + 1)
                ve.tensor_scalar(xin[:, t % 2], xin[:, t % 2], mv[:, t, 1:2], rstd[:, t:t + 1],
                                 ALU.subtract, ALU.mult).then_inc(xn1, 1)

            def turned_low(n, t, par, high_done, done):
                ve.wait_ge(high_done, RT * n + t + 1)
                low(T[:, par, 1, :, t * P:(t + 1) * P], mis[:, t % 2].rearrange("p (c r) -> p c r", c=C),
                    T[:, par, 0, :, t * P:(t + 1) * P]).then_inc(done, 1)

            stats_first(0, 0)
            stats_first(0, 1)
            ve.wait_ge(s_cols, 1)
            link(ve.tensor_copy(cols[:], hid[:, 0, 0:NV]))
            link(ve.tensor_scalar(kth[:], phase[:], float(TURN), ROUND, ALU.mult, ALU.add))
            link(ve.tensor_scalar(kth[:], kth[:], -ROUND, None, ALU.add))
            for part in (TP1, TP2, TP3):
                link(ve.scalar_tensor_tensor(out=phase[:], in0=kth[:], scalar=-part, in1=phase[:],
                                             op0=ALU.mult, op1=ALU.add))
            link(ve.tensor_scalar(arg[:, 0], phase[:], PI_BELOW, -PI_BELOW, ALU.min, ALU.max))
            link(ve.scalar_tensor_tensor(out=arg[:, 1], in0=arg[:, 0], scalar=-1.0, in1=arg[:, 0],
                                         op0=ALU.mult, op1=ALU.max))
            link(ve.tensor_scalar(arg[:, 1], arg[:, 1], -1.0, float(np.pi / 2), ALU.mult, ALU.add))
            ve.tensor_scalar(kth[:], b1c[:], HSCALE, None, ALU.mult).then_inc(s_args, 1)
            ve.wait_ge(s_args, 1)
            link(ve.scalar_tensor_tensor(out=hbias[:], in0=phase[:], scalar=float(TURN), in1=kth[:],
                                         op0=ALU.mult, op1=ALU.add))
            ve.wait_ge(s_trig, 1)
            link(ve.tensor_tensor(camp[:], trig[:, 1], wre[:], ALU.mult))
            link(ve.tensor_tensor(kth[:], trig[:, 0], wim[:], ALU.mult))
            link(ve.tensor_tensor(camp[:], camp[:], kth[:], ALU.add))
            link(ve.scalar_tensor_tensor(out=camp[:], in0=camp[:], scalar=0.1, in1=wim[:],
                                         op0=ALU.mult, op1=ALU.mult))
            norm_first(0, 0)
            norm_first(0, 1)
            for c in range(C):
                ve.wait_ge(s_w1q_hi, c + 1)
                low(w1q[:, 1, c], w1q_raw[:, c], w1q[:, 0, c]).then_inc(s_w1q_lo, 1)
            stats_first(0, 2)
            stats_first(0, 3)
            turned_low(0, 0, 0, t1_hi, t1_lo)
            turned_low(0, 1, 0, t1_hi, t1_lo)
            norm_first(0, 2)
            norm_first(0, 3)
            turned_low(0, 2, 0, t1_hi, t1_lo)
            turned_low(0, 3, 0, t1_hi, t1_lo)
            def low_parts(s, i, q, last):
                ve.wait_ge(c_raw[q], 16 * i + 16)
                need(ve, c_stored[q], 80 * i)
                need(ve, c_vr, s)
                ve.tensor_tensor_reduce(out=tmp_w[0:CR], in0=c_rows[q], in1=e_bc[0:CR], scale=1.0, scalar=0.0,
                                        op0=ALU.mult, op1=ALU.add, accum_out=vraw[0:CR, q:q + 1]
                                        ).then_inc(c_vr, 1)
                ve.wait_ge(c_g, C * s + 2)
                low(c_turned[q][:, 1], mis[:, q, 0:C * CR], c_turned[q][:, 0]).then_inc(c_tlo, 1)
                ve.wait_ge(c_vr, s + 1)
                ve.tensor_tensor(vsum[0:CR, q:q + 1], vraw[0:CR, q:q + 1], bsim[0:CR], ALU.add).then_inc(c_v, 1)
                for c in range(2, C):
                    ve.tensor_scalar(c_gfull[q][:, c * CR:(c + 1) * CR], mis[:, q, c * CR:(c + 1) * CR],
                                     w3c[:, c:c + 1], w1c[:, c:c + 1], ALU.mult, ALU.add).then_inc(c_g, 1)
                ve.wait_ge(c_ghi, s + 1)
                low(c_gsplit[q][:, 1], c_gfull[q], c_gsplit[q][:, 0]).then_inc(c_glo, 1)
                ve.wait_ge(c_whi, s + 1)
                low(c_product[q][:, 1], hid[0:CR, q], c_product[q][:, 0]).then_inc(c_wlo, 1)

            context_steps(ve, low_parts)
            ve.wait_ge(s_w03, 32)

            def sine_term(g, f):
                ve.wait_ge(s_done, g + 1)
                ve.scalar_tensor_tensor(out=h2[:, f % 2], in0=ph[:, f % 2], scalar=camp[:, f:f + 1],
                                        in1=h2[:, f % 2], op0=ALU.mult, op1=ALU.add).then_inc(q_done, 1)

            def reduce_phase(b, f):
                g = FT * b + f
                ve.wait_ge(t_done, g + 1)
                need(ve, r_done, g)
                ve.tensor_scalar(kk[:], ph[:, f % 2], ROUND, -ROUND, ALU.add, ALU.add).then_inc(k_done, 1)
                ve.wait_ge(k_done, g + 1)
                ve.tensor_tensor(ph[:, f % 2], ph[:, f % 2], kk[:], ALU.subtract).then_inc(r_done, 1)

            def relu_low(g, f):
                ve.wait_ge(act_hi, g + 1)
                ve.scalar_tensor_tensor(out=act[:, f % 4, 1], in0=h2[:, f % 2], scalar=0.0,
                                        in1=act[:, f % 4, 0].bitcast(F32), op0=ALU.max, op1=ALU.subtract
                                        ).then_inc(act_lo, 1)

            def row_max(n):
                ve.wait_ge(simr_done, n + 1)
                s = mis[:, 1, 0:RT * J].rearrange("p (t j) -> p t j", t=RT)
                ve.tensor_reduce(rmax[:], s, AX.X, ALU.max).then_inc(rmax_done, 1)
                ve.wait_ge(rmax_done, n + 1)
                ve.tensor_tensor(prob[:], s, rmax[:].unsqueeze(2).to_broadcast([P, RT, J]), ALU.subtract
                                 ).then_inc(shift_done, 1)

            def probabilities(n):
                ve.wait_ge(mbc_done, n + 1)
                ve.tensor_reduce(gmax[:], mis[:, 0], AX.X, ALU.max, negate=True).then_inc(gmax_done, 1)
                ve.wait_ge(exp_done, n + 1)
                ve.tensor_reduce(rsum[:], prob[:], AX.X, ALU.add).then_inc(rsum_done, 1)
                ve.wait_ge(rsum_done, n + 1)
                ve.reciprocal(rrec[:], rsum[:]).then_inc(rrec_done, 1)
                ve.wait_ge(rrec_done, n + 1)
                ve.tensor_tensor(prob[:], prob[:], rrec[:].unsqueeze(2).to_broadcast([P, RT, J]), ALU.mult
                                 ).then_inc(prob_done, 1)
                ve.wait_ge(ebc_done, n + 1)
                ve.reciprocal(erec[:], esum[:]).then_inc(erec_done, 1)

            def prob_low(n):
                ve.wait_ge(at_hi, n + 1)
                low(at_s[:, 1], mis[0:J, 1], at_s[:, 0]).then_inc(at_lo, 1)

            def row_mean(n):
                for c in range(C):
                    ve.wait_ge(full_done, C * n + c + 1)
                    need(ve, w0_lo if c == 0 else hbr_done, C * n + c)
                    ve.tensor_tensor_reduce(out=tmp_w[:], in0=full[:, c], in1=e_bc[:], scale=1.0, scalar=0.0,
                                            op0=ALU.mult, op1=ALU.add, accum_out=hb_raw[:, c:c + 1]
                                            ).then_inc(hbr_done, 1)
                ve.wait_ge(hbr_done, C * (n + 1))
                ve.wait_ge(erec_done, n + 1)
                ve.tensor_scalar(hb[:], hb_raw[:], erec[:], None, ALU.mult).then_inc(hb_done, 1)

            def w0_chunk(n, c):
                if c == 0:
                    ve.wait_ge(hb_done, n + 1)
                need(ve, w0_lo, C * n + c)
                ve.scalar_tensor_tensor(out=tmp_w[:], in0=w3_sb[:, c], scalar=hb[:, c:c + 1], in1=w0_sb[:, c],
                                        op0=ALU.mult, op1=ALU.add).then_inc(w0t_done, 1)

            def w0_low(n, c):
                ve.wait_ge(w0_hi, C * n + c + 1)
                low(w0s[:, c % 2, 1], tmp_w[:], w0s[:, c % 2, 0]).then_inc(w0_lo, 1)

            def pr_chunk(n, c):
                ve.wait_ge(hqh_done, C * n + c + 1)
                ve.tensor_tensor(full[:, c], mis[:, c % 2], full[:, c], ALU.mult).then_inc(prt_done, 1)

            def pr_low_(n, c):
                ve.wait_ge(pr_hi, C * n + c + 1)
                low(prs[:, c % 2, 1], full[:, c], prs[:, c % 2, 0]).then_inc(pr_lo, 1)

            def chunk(n, c):
                if c >= 2:
                    ve.wait_ge(chunk_done, (C - 1) * n + c - 1)
                w0_chunk(n, c)
                pr_chunk(n, c)
                w0_low(n, c)
                pr_low_(n, c)

            def evacuate(par, t, done):
                ve.tensor_tensor(X[:, par, t], X[:, par, t], acc[:, t], ALU.add).then_inc(done, 1)

            def add_attention(n, par):
                ve.wait_ge(xb_done, n + 1)
                for t in range(RT):
                    ve.wait_ge(att_done, RT * n + t + 1)
                    evacuate(par, t, x2_done)

            def stats_second(n, par):
                for t in range(RT):
                    ve.wait_ge(x2_done, RT * n + t + 1)
                    ve.bn_stats(st[:, t], X[:, par, t]).then_inc(st2, 1)

            def norm_second(n, par, t):
                ve.wait_ge(rs2, n + 1)
                if t >= 2:
                    ve.wait_ge(tr2, RT * n + t - 1)
                ve.tensor_scalar(xin[:, t % 2], X[:, par, t], mv[:, t, 1:2], rstd[:, t:t + 1],
                                 ALU.subtract, ALU.mult).then_inc(xn2, 1)

            def add_first_part(b, par):
                ve.wait_ge(xb2_done, b + 1)
                ve.wait_ge(ffn2_done, FT * b + NA - LAG)
                for t in range(RT):
                    evacuate(par, t, a_evac)

            def add_last_part(b, par, whole):
                ve.wait_ge(ffn2_done, FT * (b + 1))
                if whole:
                    ve.wait_ge(xb2_done, b + 1)
                else:
                    ve.wait_ge(a_evac, RT * (b + 1))
                for t in range(RT):
                    evacuate(par, t, b_evac)

            def attention_first():
                row_max(0)
                probabilities(0)
                prob_low(0)
                row_mean(0)
                for c in range(C):
                    chunk(0, c)
                add_attention(0, 0)
                stats_second(0, 0)
                for t in range(RT):
                    norm_second(0, 0, t)
                    if t >= 1:
                        turned_low(0, t - 1, 0, t2_hi, t2_lo)
                turned_low(0, RT - 1, 0, t2_hi, t2_lo)

            def body(b, par, first, last):
                n, pn = b + 1, 1 - par
                for f in range(FT):
                    g = FT * b + f
                    if f == NA and not last:
                        add_first_part(b, par)
                    if f == 3 and not first:
                        add_last_part(b - 1, pn, False)
                    if f == 0 and not last:
                        stats_first(n, 0)
                        stats_first(n, 1)
                    if f == 1 and not last:
                        norm_first(n, 0)
                        norm_first(n, 1)
                    if f == 3 and not last:
                        norm_first(n, 2)
                        norm_first(n, 3)
                    if f == NA + 1 and not last:
                        stats_second(n, pn)
                    if f == NA + 3 and not last:
                        norm_second(n, pn, 0)
                        norm_second(n, pn, 1)
                    if f == NA + 4 and not last:
                        norm_second(n, pn, 2)
                        norm_second(n, pn, 3)
                    reduce_phase(b, f)
                    if f > 0 or not first:
                        sine_term(g - 1, (f - 1) % FT)
                        relu_low(g - 1, (f - 1) % FT)
                    if last:
                        continue
                    if f == 1:
                        turned_low(n, 0, pn, t1_hi, t1_lo)
                        turned_low(n, 1, pn, t1_hi, t1_lo)
                    if f == 2:
                        stats_first(n, 2)
                        stats_first(n, 3)
                    if f == 3:
                        turned_low(n, 2, pn, t1_hi, t1_lo)
                        turned_low(n, 3, pn, t1_hi, t1_lo)
                    if f == 5:
                        row_max(n)
                    if f == 6:
                        probabilities(n)
                    if f == 7:
                        prob_low(n)
                    if f == NA - 2:
                        row_mean(n)
                    if f == NA - 1:
                        chunk(n, 0)
                    if f == NA:
                        for c in range(1, C):
                            chunk(n, c)
                        add_attention(n, pn)
                    if f == NA + 3:
                        turned_low(n, 0, pn, t2_hi, t2_lo)
                        turned_low(n, 1, pn, t2_hi, t2_lo)
                    if f == NA + 4:
                        turned_low(n, 2, pn, t2_hi, t2_lo)
                        turned_low(n, 3, pn, t2_hi, t2_lo)

            def rest():
                g = FT * B - 1
                sine_term(g, FT - 1)
                relu_low(g, FT - 1)
                add_last_part(B - 1, (B - 1) % 2, True)

            batches(ve, attention_first, body, rest)

        @block.gpsimd
        def _(po):
            po.memset(ident[:], 0.0).then_inc(s_ident0, 1)
            po.memset(mhalf[:], -0.5).then_inc(s_mhalf, 1)
            po.memset(eps_t[:], EPS).then_inc(s_mhalf, 1)
            po.memset(quarter[:], 0.25).then_inc(s_mhalf, 1)
            po.memset(ones[:], 1.0).then_inc(s_mhalf, 1)
            po.memset(mscale[:, :, 0:2], 0.5).then_inc(s_mhalf, 1)
            po.memset(mscale[:, :, 2:3], 1.0 / D).then_inc(s_mhalf, 1)
            po.wait_ge(s_ident0, 1)
            po.affine_select(out=ident[:], in_=ident[:], compare_op=ALU.not_equal, fill=1.0, base=0,
                             pattern=[[-1, P]], channel_multiplier=1).then_inc(s_ident, 1)
            po.wait_ge(s_mhalf, 6)

            def w1_low(g, f):
                po.wait_ge(w1_hi, g + 1)
                po.tensor_tensor(w1s[:, f % 2, 1], w1_sb[:, :, f * P:(f + 1) * P], w1s[:, f % 2, 0].bitcast(F32),
                                 ALU.subtract).then_inc(w1_lo, 1)

            def moments(t0, t1, stats_done, stats_count, step, count, done):
                po.wait_ge(stats_done, stats_count)
                halves = st[:, t0:t1].rearrange("p t (h k) -> p t h k", h=2)
                po.tensor_tensor(mv[:, t0:t1], halves[:, :, 0], halves[:, :, 1], ALU.add).then_inc(step, 1)
                po.tensor_tensor(dev[:, t0:t1], halves[:, :, 0, 1], halves[:, :, 1, 1], ALU.subtract).then_inc(step, 1)
                po.wait_ge(step, count - 3)
                po.tensor_tensor(mv[:, t0:t1], mv[:, t0:t1], mscale[:, t0:t1], ALU.mult).then_inc(step, 1)
                po.tensor_tensor(dev[:, t0:t1], dev[:, t0:t1], dev[:, t0:t1], ALU.mult).then_inc(step, 1)
                po.wait_ge(step, count - 1)
                po.tensor_tensor(dev[:, t0:t1], dev[:, t0:t1], quarter[:, t0:t1], ALU.mult).then_inc(step, 1)
                po.wait_ge(step, count)
                po.tensor_tensor(vareps[:, t0:t1], mv[:, t0:t1, 2], dev[:, t0:t1], ALU.add).then_inc(step, 1)
                po.wait_ge(step, count + 1)
                po.tensor_tensor(vareps[:, t0:t1], vareps[:, t0:t1], eps_t[:, t0:t1], ALU.add).then_inc(step, 1)
                po.wait_ge(step, count + 2)
                po.tensor_tensor(rstd[:, t0:t1], vareps[:, t0:t1], mhalf[:, t0:t1], ALU.pow).then_inc(done, 1)

            def deviation_first(n, half):
                moments(2 * half, 2 * half + 2, st1, RT * n + 2 * half + 2, mo1, 7 * (2 * n + half) + 5, rs1)

            def deviation_second(n):
                moments(0, RT, st2, RT * (n + 1), mo2, 7 * n + 5, rs2)

            def whole(n, c, par):
                if c == 0:
                    need(po, pr_lo, C * n)
                    po.wait_ge(t1_lo, RT * (n + 1))
                po.tensor_tensor(full[:, c], T[:, par, 0, c].bitcast(F32), T[:, par, 1, c].bitcast(F32), ALU.add
                                 ).then_inc(full_done, 1)

            def weight_split(k, q, i):
                po.wait_ge(r_raw[q], 16 * i + 16)
                need(po, r_stored[q], 16 * i)
                po.tensor_tensor(w2s[:, q, 0], w_raw[q], ones[:].to_broadcast([P, D]), ALU.mult).then_inc(r_hi, 1)
                po.wait_ge(r_hi, k + 1)
                po.tensor_tensor(w2s[:, q, 1], w_raw[q], w2s[:, q, 0].bitcast(F32), ALU.subtract).then_inc(r_lo, 1)

            def rows_low(s, i, q, last):
                po.wait_ge(c_hqhi, s + 1)
                po.tensor_tensor(c_split[q][:, 1], c_rows[q], c_split[q][:, 0].bitcast(F32), ALU.subtract
                                 ).then_inc(c_hqlo, 1)
                weight_split(s, q, i)

            def add_bqv(n, par):
                po.wait_ge(x_in, 16 * (n + 1))
                po.tensor_tensor(X[:, par], X[:, par], bqv_bc[:].unsqueeze(1).to_broadcast([P, RT, D]), ALU.add
                                 ).then_inc(xb_done, 1)

            def add_b2(n, par):
                po.wait_ge(xn2, RT * (n + 1))
                po.tensor_tensor(X[:, par], X[:, par], b2_bc[:].unsqueeze(1).to_broadcast([P, RT, D]), ALU.add
                                 ).then_inc(xb2_done, 1)

            deviation_first(0, 0)
            deviation_first(0, 1)
            po.wait_ge(s_const, 160)
            context_steps(po, rows_low)

            def attention_first():
                for k in range(CN, CN + C):
                    weight_split(k, k % 2, k // 2)
                for c in range(C):
                    whole(0, c, 0)
                for k in range(CN + C, CN + len(LATE)):
                    weight_split(k, k % 2, k // 2)
                    if k == CN + C + 2:
                        add_bqv(0, 0)
                deviation_second(0)
                add_b2(0, 0)
                po.wait_ge(s_w1, 16)
                w1_low(0, 0)
                w1_low(1, 1)

            def body(b, par, first, last):
                n, pn = b + 1, 1 - par
                for f in range(FT):
                    g = FT * b + f
                    if f == 0 and not last:
                        deviation_first(n, 0)
                    if f < FT - 2 or not last:
                        w1_low(g + 2, (f + 2) % FT)
                    if last:
                        continue
                    if f == 2:
                        deviation_first(n, 1)
                    if f in (4, 5):
                        for c in range(2):
                            whole(n, 2 * (f - 4) + c, pn)
                    if f == NA - 3:
                        add_bqv(n, pn)
                    if f == NA + 1:
                        deviation_second(n)
                    if f == NA + 4:
                        add_b2(n, pn)

            batches(po, attention_first, body, lambda: None)


_INS = ['x', 'ctx_1024', 'L0_xattn_w_sim', 'L0_xattn_b_sim', 'L0_xattn_W_qv', 'L0_xattn_b_qv', 'L0_ffn_W1', 'L0_ffn_b1',
        'L0_ffn_quantum_phases', 'L0_ffn_quantum_weights_real', 'L0_ffn_quantum_weights_imag', 'L0_ffn_W2', 'L0_ffn_b2']


def kernel(**inputs):
    import numpy as _np
    import concourse.bacc as _bacc
    from concourse import mybir as _mybir
    from concourse.bass_utils import run_bass_kernel_spmd as _run

    nc = _bacc.Bacc("TRN2", target_bir_lowering=False, num_devices=1)
    arrays, args = {}, []
    for name in _INS:
        a = _np.ascontiguousarray(inputs[name])
        arrays[f"in_{name}"] = a
        args.append(nc.dram_tensor(f"in_{name}", a.shape, _mybir.dt.from_np(a.dtype), kind="ExternalInput").ap())
    shape = inputs['x'].shape
    args.append(nc.dram_tensor("out_x", shape, _mybir.dt.float32, kind="ExternalOutput").ap())
    xattn_ffn(nc, *args)
    r = _run(nc, [arrays], core_ids=[0])
    return r.results[0]["out_x"]
```

```python
from contextlib import ExitStack

import numpy as np

import concourse.bass as bass
from concourse import mybir

ALU = mybir.AluOpType
ACT = mybir.ActivationFunctionType
AX = mybir.AxisListType
F32 = mybir.dt.float32
F32R = mybir.dt.float32r

P = 128
TWO_PI = 2 * np.pi
TURN = 1 / TWO_PI
TWO_PI_BELOW = float(np.nextafter(np.float32(TWO_PI), np.float32(0)))
PI_BELOW = float(np.nextafter(np.float32(np.pi), np.float32(0)))
ROUND = 1.5 * 2.0 ** 23
TP1 = 6.28125
TP2 = float(np.float32(np.round((TWO_PI - TP1) * 2 ** 20) / 2 ** 20))
TP3 = float(np.float32(TWO_PI - TP1 - TP2))
EPS = 1e-5


def xattn_ffn(nc, x, ctx_rows, w_sim, b_sim, W_qv, b_qv, W1, b1, theta, w_real, w_imag, W2, b2, out):
    B, R, D = x.shape
    J = ctx_rows.shape[1]
    F = W1.shape[1]
    C = D // P
    RT = R // P
    FT = F // P
    CR = 112
    CN = B * J // CR
    JA = P - J
    JB = 2 * J - JA
    LATE = 4
    TAIL = 64
    NV = 4 * FT + 2 * C
    LAG = 3
    NA = 10
    HSCALE = float(0.1 * TURN)
    assert R == 512 and D == 512 and CN * CR == B * J and (CN - LATE) % 2 == 1 and FT % 4 == 0 and B % 2 == 0
    assert TAIL <= J and 2 * J >= P and JB <= P

    x_rows = x.rearrange("b (t p) d -> b p t d", p=P)
    out_rows = out.rearrange("b (t p) d -> b p t d", p=P)
    ctx_flat = ctx_rows.rearrange("b j d -> (b j) d")
    w1_dram = W1.rearrange("(c p) f -> p c f", p=P)
    w2_dram = W2.rearrange("(f p) d -> f p d", p=P)
    wqv_dram = W_qv.rearrange("(q c p) d -> q p c d", q=4, p=P)

    g_dram = nc.dram_tensor("g_dram", [P, C, B * J], F32).ap()
    hqw_dram = nc.dram_tensor("hqw_dram", [B * J, D], F32).ap()
    v_dram = nc.dram_tensor("v_dram", [B * J, 1], F32).ap()

    with ExitStack() as ctx:
        def sb(name, shape, dt=F32):
            return ctx.enter_context(nc.sbuf_tensor(name, shape, dt))

        def psum(name, shape):
            return ctx.enter_context(nc.psum_tensor(name, shape, F32))

        def sem(name):
            return ctx.enter_context(nc.semaphore(name))

        acc = psum("acc", [P, RT, D])
        hid = psum("hid", [P, 2, R])
        mis = psum("mis", [P, 2, 512])

        w1_sb = sb("w1_sb", [P, C, F])
        w1s = sb("w1s", [P, 2, 2, C, P], F32R)
        w_raw = sb("w_raw", [P, 2, D])
        ws = sb("ws", [P, 5, 2, D], F32R)
        w0_sb = sb("w0_sb", [P, C, D])
        w3_sb = sb("w3_sb", [P, C, D])
        T = sb("T", [P, 2, 2, C, R], F32R)
        X = sb("X", [P, 2, RT, D])
        xin = sb("xin", [P, 2, D])
        h2 = sb("h2", [P, 2, R])
        ph = sb("ph", [P, 2, R])
        kk = sb("kk", [P, R])
        act = sb("act", [P, 4, 2, R], F32R)
        prs = sb("prs", [P, 2, 2, R], F32R)
        w0s = sb("w0s", [P, 2, 2, D], F32R)
        full = sb("full", [P, C, R])
        hq_raw, hqw_raw, hq_tail, hqw_tail = (full[:, c] for c in range(4))
        tmp_w = sb("tmp_w", [P, D])
        bqv_bc = sb("bqv_bc", [P, D])
        b2_bc = sb("b2_bc", [P, D])
        simt = tmp_w[0:J]
        g_raw = tmp_w[:, 0:C * J]
        prob = sb("prob", [P, RT, J])
        at_s = sb("at_s", [P, 2, R], F32R)
        assert 2 * J + JB == 4 * J - JA
        split_prob = prs[:].rearrange("p a b r -> p (a b r)")[:, 0:RT * (2 * J + JB)].rearrange(
            "p (t k) -> p t k", t=RT)
        split_high = [split_prob[:, :, 2 * k * J:(2 * k + 1) * J] for k in range(2)]
        e_bc = sb("e_bc", [P, R])
        hqs = sb("hqs", [P, 2, D], F32R)
        hqw = sb("hqw", [P, 2, D], F32R)
        gs = sb("gs", [P, 2, C * J], F32R)
        ident = sb("ident", [P, P])
        vj = sb("vj", [P, 1])
        vsum = sb("vsum", [P, 2])
        cols = sb("cols", [P, NV])
        phase, wre, wim, b1c = (cols[:, k * FT:(k + 1) * FT] for k in range(4))
        w1c, w3c = (cols[:, 4 * FT + k * C:4 * FT + (k + 1) * C] for k in range(2))
        kth = sb("kth", [P, FT])
        arg = sb("arg", [P, 2, FT])
        trig = sb("trig", [P, 2, FT])
        hbias = sb("hbias", [P, FT])
        camp = sb("camp", [P, FT])
        bsim = sb("bsim", [P, 1])
        vraw = sb("vraw", [P, 2])
        st = sb("st", [P, RT, 6])
        mv = sb("mv", [P, RT, 3])
        dev = sb("dev", [P, RT])
        mscale = sb("mscale", [P, RT, 3])
        quarter = sb("quarter", [P, RT])
        ones = sb("ones", [P, 1])
        vareps = sb("vareps", [P, RT])
        mhalf = sb("mhalf", [P, RT])
        eps_t = sb("eps_t", [P, RT])
        rstd = sb("rstd", [P, RT])
        rmax = sb("rmax", [P, RT])
        rsum = sb("rsum", [P, RT])
        rrec = sb("rrec", [P, RT])
        gmax = sb("gmax", [P, 1])
        esum = sb("esum", [P, 1])
        erec = sb("erec", [P, 1])
        hb_raw = sb("hb_raw", [P, C])
        hb = sb("hb", [P, C])

        s_const = sem("s_const"); s_w1 = sem("s_w1"); s_w03 = sem("s_w03"); s_ident0 = sem("s_ident0")
        s_ident = sem("s_ident"); s_chain = sem("s_chain"); s_args = sem("s_args"); s_trig = sem("s_trig")
        s_mhalf = sem("s_mhalf"); s_cols = sem("s_cols"); s_w1q_raw = sem("s_w1q_raw")
        s_w1q_hi = sem("s_w1q_hi"); s_w1q_lo = sem("s_w1q_lo")
        c_raw = [sem(f"c_raw{i}") for i in range(2)]; c_vr = sem("c_vr"); c_v = sem("c_v")
        c_stored = [sem(f"c_stored{i}") for i in range(2)]
        p_stored = [sem(f"p_stored{i}") for i in range(2)]
        c_tr = sem("c_tr"); c_thi = sem("c_thi"); c_tlo = sem("c_tlo")
        c_ga = sem("c_ga"); c_gd = sem("c_gd"); c_mm = sem("c_mm"); c_out = sem("c_out")
        w_in = [sem(f"w_in{i}") for i in range(2)]; w_hi = sem("w_hi"); w_lo = sem("w_lo")
        w1_hi = sem("w1_hi"); w1_lo = sem("w1_lo")
        hid_done = sem("hid_done"); t_done = sem("t_done"); h2_done = sem("h2_done"); k_done = sem("k_done")
        r_done = sem("r_done"); s_done = sem("s_done"); q_done = sem("q_done")
        act_hi = sem("act_hi"); act_lo = sem("act_lo"); ffn2_done = sem("ffn2_done")
        last_sum = sem("last_sum")
        a_evac = sem("a_evac"); b_evac = sem("b_evac"); out_stored = sem("out_stored")
        ctx_in = sem("ctx_in"); xin_in = [sem(f"xin_in{i}") for i in range(2)]; x_in = sem("x_in")
        ctx_hi = sem("ctx_hi"); g_lo = sem("g_lo"); hq_lo = sem("hq_lo")
        st1 = sem("st1"); mo1 = sem("mo1"); rs1 = sem("rs1"); xn1 = sem("xn1"); tr1 = sem("tr1")
        t1_hi = sem("t1_hi"); t1_lo = sem("t1_lo"); sim_done = sem("sim_done"); simt_done = sem("simt_done")
        simr_done = sem("simr_done"); rmax_done = sem("rmax_done"); shift_done = sem("shift_done")
        exp_done = sem("exp_done"); rsum_done = sem("rsum_done"); rrec_done = sem("rrec_done")
        prob_done = sem("prob_done"); mbc_done = sem("mbc_done"); gmax_done = sem("gmax_done")
        ebc_done = sem("ebc_done"); erec_done = sem("erec_done"); at_done = sem("at_done")
        split_hi = sem("split_hi"); split_lo = sem("split_lo"); at_out = sem("at_out")
        hqh_done = sem("hqh_done"); full_done = sem("full_done")
        hbr_done = sem("hbr_done"); hb_done = sem("hb_done")
        w0t_done = sem("w0t_done"); w0_hi = sem("w0_hi"); w0_lo = sem("w0_lo")
        prt_done = sem("prt_done"); pr_hi = sem("pr_hi"); pr_lo = sem("pr_lo")
        chunk_done = sem("chunk_done"); att_done = sem("att_done")
        xb_done = sem("xb_done"); x2_done = sem("x2_done"); xb2_done = sem("xb2_done")
        st2 = sem("st2"); mo2 = sem("mo2"); rs2 = sem("rs2"); xn2 = sem("xn2"); tr2 = sem("tr2")
        t2_hi = sem("t2_hi"); t2_lo = sem("t2_lo")

        def need(eng, s, count):
            if isinstance(count, int) and count <= 0:
                return
            eng.wait_ge(s, count)

        FIRST = NA - LAG
        STREAM = FT + C
        assert STREAM % 5 == 0 and STREAM % 2 == 0 and C % 2 == 0
        SPLITS = {f + 1: [f] for f in range(FIRST)}
        SPLITS.update({NA - 2: [FIRST], NA - 1: [FIRST + 1], NA: [FIRST + 2, FIRST + 3, FIRST + 4],
                       NA + 1: [FIRST + 5, FIRST + 6], NA + 2: [FIRST + 7, FIRST + 8], NA + 3: [FIRST + 9, FIRST + 10],
                       NA + 4: [FIRST + 11], NA + 5: [FIRST + 12]})
        LAST_SPLITS = {f + 1: [f] for f in range(FT - 1)}
        LAST_SPLITS[FT - 1] = [FT - 2, FT - 1]

        def splits(f, last):
            return (LAST_SPLITS if last else SPLITS).get(f, [])

        def count_of(b, p):
            return C + STREAM * b + p

        def place_w2(f, whole):
            return f if whole or f < FIRST else f + C

        def wait_left(eng, b, p, last):
            q = p - 5
            if q < 0:
                if isinstance(b, int) and b == 0:
                    c, n = C + q, 0
                    if c < 0:
                        return
                    eng.wait_ge(chunk_done if c < C - 1 else att_done, c + 1 if c < C - 1 else RT)
                    return
                b, q, last = b - 1, q + STREAM, False
            if last or q < FIRST:
                eng.wait_ge(ffn2_done, FT * b + q + 1)
            elif q < FIRST + C - 1:
                eng.wait_ge(chunk_done, (C - 1) * (b + 1) + q - FIRST + 1)
            elif q == FIRST + C - 1:
                eng.wait_ge(att_done, RT * (b + 2))
            else:
                eng.wait_ge(ffn2_done, FT * b + q - C + 1)

        def settle(eng):
            eng.wait_ge(s_ident, 1)

        def batches(eng, attention_first, body, rest):
            attention_first()
            body(0, 0, True, False)
            with eng.Fori(0, (B - 2) // 2) as i:
                body(2 * i + 1, 1, False, False)
                body(2 * i + 2, 0, False, False)
            body(B - 1, (B - 1) % 2, False, True)
            rest()

        def context_steps(eng, step):
            for s in range(3):
                single_step(step, s)
            with eng.Fori(1, (CN - LATE) // 2) as i:
                step(2 * i + 1, i, 1)
                step(2 * i + 2, i + 1, 0)

        def single_step(step, s):
            step(s, s // 2, s % 2)

        c_rows = [h2[0:CR, q] for q in range(2)]
        c_turned = [act[:, 2 * q, :, 0:C * CR] for q in range(2)]
        c_gfull = [ph[:, q, 0:C * CR] for q in range(2)]
        c_product = [X[0:CR, 1, q] for q in range(2)]
        w1q_raw, w1q = w3_sb, T[:, 1]

        block = ctx.enter_context(nc.Block())

        @block.sync
        def _(sp):
            col = lambda v: v.rearrange("(t p) -> t p", p=P)
            at = lambda k, n: tmp_w[k:k + n, 0:P]
            row = lambda v, n: v.rearrange("(a d) -> a d", a=1).to_broadcast([n, D])

            def xin_load(n, t):
                if t < 2:
                    need(sp, tr2, RT * n - 2 + t + 1)
                else:
                    sp.wait_ge(tr1, RT * n + t - 1)
                sp.dma_start(xin[:, t % 2], x_rows[bass.ds(n, 1), :, t].rearrange("b p d -> (b p) d")
                             ).then_inc(xin_in[t % 2], 16)

            def x_load(n, par):
                need(sp, out_stored, 16 * (n - 1))
                sp.dma_start(X[:, par], x_rows[bass.ds(n, 1)].rearrange("b p t d -> (b p) t d")
                             ).then_inc(x_in, 16)

            def rows_in(s, q):
                need(sp, c_vr, s - 1)
                need(sp, c_tr, s - 1)
                sp.dma_start(c_rows[q], ctx_flat[bass.ds(s * CR, CR), :]).then_inc(c_raw[q], 16)

            x_load(0, 0)
            rows_in(0, 0)
            sp.dma_start(w1q_raw[:], wqv_dram[1]).then_inc(s_w1q_raw, 16)
            consts = [(at(0, FT), col(theta)), (at(FT, FT), col(w_real)), (at(2 * FT, FT), col(w_imag)),
                      (at(3 * FT, FT), col(b1)), (at(4 * FT, C), col(w_sim[0:D])),
                      (at(4 * FT + C, C), col(w_sim[2 * D:3 * D])),
                      (bsim[:], b_sim.rearrange("(a d) -> a d", a=1).to_broadcast([P, 1])),
                      (e_bc[:], row(w_sim[D:2 * D], P)), (bqv_bc[:], row(b_qv, P)), (b2_bc[:], row(b2, P))]
            for dst, src in consts:
                sp.dma_start(dst, src).then_inc(s_const, 16)

            def product_out(s, q):
                sp.wait_ge(c_out, s + 1)
                sp.dma_start(hqw_dram[bass.ds(s * CR, CR), :], c_product[q]).then_inc(p_stored[q], 16)

            def rows_step(s, i, q):
                if not (isinstance(s, int) and s + 2 >= CN):
                    rows_in(s + 2, q)
                rows = bass.ds(s * CR, CR)
                settle(sp)
                sp.wait_ge(c_v, s + 1)
                sp.dma_start(v_dram[rows, :], vsum[0:CR, q:q + 1]).then_inc(c_stored[q], 16)
                sp.wait_ge(c_ga, 2 * (s + 1))
                sp.wait_ge(c_gd, 2 * (s + 1))
                sp.dma_start(g_dram[:, :, rows], c_gfull[q].rearrange("p (c j) -> p c j", c=C)
                             ).then_inc(c_stored[q], 16)
                if not (isinstance(s, int) and s == 0):
                    product_out(s - 1, 1 - q)

            def ctx_load(n, parts=(0, 1)):
                rows = bass.ds(n * J, J)
                if 0 in parts:
                    if isinstance(n, int) and n == 0:
                        sp.wait_ge(s_cols, 1)
                    need(sp, pr_lo, C * n)
                    need(sp, w0_lo, C * n)
                    need(sp, att_done, RT * n)
                    sp.dma_start(g_raw.rearrange("p (c j) -> p c j", c=C), g_dram[:, :, rows]).then_inc(ctx_in, 16)
                    sp.dma_start(vj[0:J], v_dram[rows, :]).then_inc(ctx_in, 16)
                for k in parts:
                    raw, tail, src = ((hq_raw, hq_tail, ctx_flat), (hqw_raw, hqw_tail, hqw_dram))[k]
                    sp.dma_start(raw[0:J], src[rows, :]).then_inc(ctx_in, 16)
                    sp.dma_start(raw[J:P], src[bass.ds(n * J, JA), :]).then_inc(ctx_in, 16)
                    sp.dma_start(tail[TAIL:JB], src[bass.ds(n * J + JA - (J - TAIL), JB - TAIL), :]
                                 ).then_inc(ctx_in, 16)

            def tile_load(b, p, last):
                need(sp, w_lo, count_of(b, p) - 1)
                if last or p < FIRST:
                    src = w2_dram[p]
                else:
                    src = wqv_dram[2, :, p - FIRST] if p < FIRST + C else w2_dram[p - C]
                sp.dma_start(w_raw[:, p % 2], src).then_inc(w_in[p % 2], 16)

            def first_tile_load(c):
                need(sp, w_lo, c - 1)
                sp.dma_start(w_raw[:, c % 2], wqv_dram[2, :, c]).then_inc(w_in[c % 2], 16)

            for q in range(2):
                if q == 1:
                    rows_in(1, 1)
                first_tile_load(q)
            sp.wait_ge(s_w1q_lo, C)
            first_tile_load(2)
            first_tile_load(3)
            context_steps(sp, rows_step)
            sp.wait_ge(c_stored[0], 16 * 2)
            sp.wait_ge(p_stored[0], 16)
            ctx_load(0, [0])
            single_step(rows_step, CN - LATE)
            ctx_load(0, [1])
            for s in range(CN - LATE + 1, CN):
                single_step(rows_step, s)
                if s == CN - 3:
                    sp.dma_start(w3_sb[:], wqv_dram[3]).then_inc(s_w03, 16)
                    sp.dma_start(w0_sb[:], wqv_dram[0]).then_inc(s_w03, 16)
            product_out(CN - 1, (CN - 1) % 2)

            def store(b, par):
                sp.wait_ge(b_evac, RT * (b + 1))
                sp.dma_start(out_rows[bass.ds(b, 1)].rearrange("b p t d -> (b p) t d"), X[:, par]
                             ).then_inc(out_stored, 16)

            def attention_first():
                sp.dma_start(w1_sb[:], w1_dram).then_inc(s_w1, 16)
                for q in range(2):
                    sp.wait_ge(c_stored[q], 16 * 2 * ((CN + 1 - q) // 2))
                    sp.wait_ge(p_stored[q], 16 * ((CN + 1 - q) // 2))

            def body(b, par, first, last):
                n, pn = b + 1, 1 - par
                for f in range(FT):
                    if f == 0 and not last:
                        xin_load(n, 0)
                        xin_load(n, 1)
                    if f == 0:
                        tile_load(b, 0, last)
                        if not last:
                            ctx_load(n)
                    for p in splits(f, last):
                        if p + 1 < (FT if last else STREAM):
                            tile_load(b, p + 1, last)
                    if f == 4 and not first:
                        store(b - 1, pn)
                    if last:
                        continue
                    if f == 1:
                        xin_load(n, 2)
                        xin_load(n, 3)
                    if f == 6:
                        x_load(n, pn)

            def rest():
                for t in range(RT):
                    sp.wait_ge(b_evac, RT * (B - 1) + t + 1)
                    sp.dma_start(out_rows[B - 1, :, t], X[:, (B - 1) % 2, t]).then_inc(out_stored, 16)
                sp.wait_ge(out_stored, 16 * (B - 1 + RT))

            batches(sp, attention_first, body, rest)

        @block.tensor
        def _(pe):
            def three(dst, w_hi, w_lo, m_hi, m_lo, start, stop, done=None):
                pe.matmul(dst, w_hi, m_hi, start=start, stop=False)
                pe.matmul(dst, w_hi, m_lo, start=False, stop=False)
                mm = pe.matmul(dst, w_lo, m_hi, start=False, stop=stop)
                if done is not None:
                    mm.then_inc(done, 1)

            def stacked(dst, w, m, start, stop, done=None):
                pe.matmul(dst, w(P, 0), m(P, 0), start=start, stop=False)
                mm = pe.matmul(dst, w(JB, 1), m(JB, 1), start=False, stop=stop)
                if done is not None:
                    mm.then_inc(done, 1)

            def turn_vectors():
                pe.wait_ge(s_const, 160)
                pe.transpose(hid[:, 0, 0:NV], tmp_w[0:NV, 0:P], ident[0:NV, 0:NV]).then_inc(s_cols, 1)

            def turn(s, i, q):
                pe.wait_ge(c_raw[q], 16 * i + 16)
                if not (isinstance(s, int) and s < 2):
                    pe.wait_ge(c_tlo, s - 1)
                    pe.wait_ge(c_gd, 2 * (s - 1))
                for c in range(C):
                    tr = pe.transpose(acc[:, q, c * CR:(c + 1) * CR], c_rows[q][:, c * P:(c + 1) * P],
                                      ident[0:CR, 0:CR])
                tr.then_inc(c_tr, 1)

            def turn_and_multiply(s, i, q):
                if not (isinstance(s, int) and s == CN - 1):
                    turn(s + 1, i + q, 1 - q)
                if isinstance(s, int) and s in (CN - LATE, CN - LATE + 1):
                    tr_first(0, s - (CN - LATE) + 2)
                pe.wait_ge(c_tlo, s + 1)
                if not (isinstance(s, int) and s < 2):
                    pe.wait_ge(c_out, s - 1)
                for c in range(C):
                    hq = c_turned[q][:, :, c * CR:(c + 1) * CR]
                    w = w1q[:, :, c]
                    three(hid[0:CR, q], hq[:, 0], hq[:, 1], w[:, 0], w[:, 1], c == 0, c == C - 1,
                          c_mm if c == C - 1 else None)

            def hidden(b, f, par):
                g = FT * b + f
                pe.wait_ge(w1_lo, g + 1)
                need(pe, h2_done, g - 1)
                if f == 0:
                    pe.wait_ge(t2_lo, RT * (b + 1))
                w = w1s[:, f % 2]
                for c in range(C):
                    three(hid[:, f % 2], w[:, 0, c], w[:, 1, c], T[:, par, 0, c], T[:, par, 1, c],
                          c == 0, c == C - 1, hid_done if c == C - 1 else None)

            def second(b, f, whole):
                g = FT * b + f
                pe.wait_ge(act_lo, g + 1)
                p = place_w2(f, whole)
                pe.wait_ge(w_lo, count_of(b, p) + 1)
                w = ws[:, (C + p) % 5]
                begins = f == 0 or (f == NA - 3 and not whole)
                ends = f == FT - 1 or (f == NA - 4 and not whole)
                for t in range(RT):
                    if f == 0:
                        need(pe, b_evac, RT * (b - 1) + t + 1)
                    if f == NA - 3 and not whole:
                        pe.wait_ge(x2_done, RT * (b + 1) + t + 1)
                    a = act[:, f % 4, :, t * P:(t + 1) * P]
                    if f == FT - 1 and whole:
                        done = last_sum
                    else:
                        done = ffn2_done if t == RT - 1 else None
                    three(acc[:, t], a[:, 0], a[:, 1], w[:, 0], w[:, 1], begins, ends, done)

            def transpose_rows(n, t, ready, done, left):
                pe.wait_ge(ready, RT * n + t + 1)
                need(pe, *left)
                for c in range(C):
                    tr = pe.transpose(mis[:, t % 2, c * P:(c + 1) * P], xin[:, t % 2, c * P:(c + 1) * P], ident[:])
                tr.then_inc(done, 1)

            def tr_first(n, t):
                transpose_rows(n, t, xn1, tr1, (t2_lo, RT * n - 2 + t + 1) if t < 2 else (t1_lo, RT * n + t - 1))

            def tr_second(n, t):
                transpose_rows(n, t, xn2, tr2, (prt_done, C * n + 3 + t) if t < 2 else (t2_lo, RT * n + t - 1))

            def sim(n, par):
                pe.wait_ge(g_lo, n + 1)
                pe.wait_ge(t1_lo, RT * (n + 1))
                for c in range(C):
                    g = gs[:, :, c * J:(c + 1) * J]
                    three(mis[0:J, 0], g[:, 0], g[:, 1], T[:, par, 0, c], T[:, par, 1, c],
                          c == 0, c == C - 1, sim_done if c == C - 1 else None)

            def sim_rows(n):
                pe.wait_ge(simt_done, n + 1)
                for t in range(RT):
                    tr = pe.transpose(mis[:, 1, t * J:(t + 1) * J], simt[:, t * P:(t + 1) * P], ident[0:J, 0:J])
                tr.then_inc(simr_done, 1)

            def spread_max(n):
                pe.wait_ge(rmax_done, n + 1)
                for t in range(RT):
                    tr = pe.transpose(mis[:, 0, t * P:(t + 1) * P], rmax[:, t:t + 1].to_broadcast([P, P]), ident[:])
                tr.then_inc(mbc_done, 1)

            def prob_turn(n):
                pe.wait_ge(split_lo, 2 * (n + 1))
                pe.wait_ge(ebc_done, n + 1)
                for t in range(RT):
                    rows = slice(t * P, (t + 1) * P)
                    pe.transpose(mis[:, 1, rows], split_prob[:, t, 0:P].bitcast(F32), ident[:])
                    tr = pe.transpose(mis[0:JB, 0, rows], split_prob[:, t, 2 * J:2 * J + JB].bitcast(F32), ident[:])
                tr.then_inc(at_done, 1)

            def hq_hat(n, c):
                if c == 0:
                    pe.wait_ge(at_out, 2 * (n + 1))
                    pe.wait_ge(hq_lo, 2 * (n + 1))
                if c >= 2:
                    pe.wait_ge(prt_done, C * n + c - 1)
                stacked(mis[:, c % 2], lambda k, a: hqs[0:k, a, c * P:(c + 1) * P], lambda k, a: at_s[0:k, a],
                        True, True, hqh_done)

            def products(n, par, first):
                hq_hat(n, 1)
                for t in range(RT):
                    if not first:
                        pe.wait_ge(a_evac, RT * (n - 1) + t + 1)
                    stacked(acc[:, t], lambda k, a: at_s[0:k, a, t * P:(t + 1) * P], lambda k, a: hqw[0:k, a],
                            True, False)
                for c in range(C):
                    pe.wait_ge(w0_lo, C * n + c + 1)
                    for t in range(RT):
                        a = T[:, par, :, c, t * P:(t + 1) * P]
                        w = w0s[:, c % 2]
                        three(acc[:, t], a[:, 0], a[:, 1], w[:, 0], w[:, 1], False, False)
                        if c == C - 1:
                            product_tile(n, c, t)
                    if c < C - 1:
                        for t in range(RT):
                            product_tile(n, c, t)
                    if c + 2 < C:
                        hq_hat(n, c + 2)

            def product_tile(n, c, t):
                if t == 0:
                    pe.wait_ge(pr_lo, C * n + c + 1)
                    at_start = isinstance(n, int) and n == 0
                    pe.wait_ge(w_lo, (c if at_start else count_of(n - 1, FIRST + c)) + 1)
                a = prs[:, c % 2, :, t * P:(t + 1) * P]
                w = ws[:, c % 5 if isinstance(n, int) and n == 0 else (C + FIRST + c) % 5]
                three(acc[:, t], a[:, 0], a[:, 1], w[:, 0], w[:, 1], False, c == C - 1,
                      att_done if c == C - 1 else (chunk_done if t == RT - 1 else None))

            pe.wait_ge(s_ident, 1)
            tr_first(0, 0)
            tr_first(0, 1)
            turn(0, 0, 0)
            turn_vectors()
            pe.wait_ge(s_w1q_lo, C)
            context_steps(pe, turn_and_multiply)

            def attention_first():
                for s in range(CN - LATE, CN - 2):
                    single_step(turn_and_multiply, s)
                sim(0, 0)
                single_step(turn_and_multiply, CN - 2)
                sim_rows(0)
                spread_max(0)
                single_step(turn_and_multiply, CN - 1)
                prob_turn(0)
                hq_hat(0, 0)
                pe.wait_ge(c_gd, 2 * CN)
                pe.wait_ge(c_out, CN)
                products(0, 0, True)
                for t in range(RT):
                    tr_second(0, t)

            def body(b, par, first, last):
                n, pn = b + 1, 1 - par
                for f in range(FT):
                    if f != NA + 1 or last:
                        hidden(b, f, par)
                    if f == 1 and not last:
                        tr_first(n, 0)
                        tr_first(n, 1)
                    if f == 6 and not last:
                        spread_max(n)
                    if f == 8 and not last:
                        prob_turn(n)
                    if f == NA - 1 and not last:
                        hq_hat(n, 0)
                    if f == NA and not last:
                        hidden(b, f + 1, par)
                        products(n, pn, False)
                        continue
                    if f == NA + 1 and not last:
                        continue
                    if f == NA + 2 and not last:
                        second(b, NA - LAG, False)
                        second(b, NA - LAG + 1, False)
                    if f >= LAG:
                        second(b, f - LAG, last)
                    elif not first:
                        second(b - 1, FT + f - LAG, False)
                    if last:
                        continue
                    if f == 3:
                        tr_first(n, 2)
                        tr_first(n, 3)
                    if f == 4:
                        sim(n, pn)
                    if f == 5:
                        sim_rows(n)
                    if f == NA + 3:
                        tr_second(n, 0)
                        tr_second(n, 1)
                    if f == NA + 4:
                        tr_second(n, 2)
                        tr_second(n, 3)

            def rest():
                for f in range(FT - LAG, FT):
                    second(B - 1, f, True)

            batches(pe, attention_first, body, rest)

        @block.scalar
        def _(sc):
            def turned_high(n, t, par, ready, done):
                sc.wait_ge(ready, RT * n + t + 1)
                nc.scalar.copy(T[:, par, 0, :, t * P:(t + 1) * P],
                               mis[:, t % 2].rearrange("p (c r) -> p c r", c=C)).then_inc(done, 1)

            for c in range(C):
                if c == 0:
                    sc.wait_ge(s_w1q_raw, 16)
                nc.scalar.copy(w1q[:, 0, c], w1q_raw[:, c]).then_inc(s_w1q_hi, 1)
            turned_high(0, 0, 0, tr1, t1_hi)
            turned_high(0, 1, 0, tr1, t1_hi)

            def product_copy(s, i, q):
                sc.wait_ge(c_mm, s + 1)
                need(sc, p_stored[q], 16 * i)
                nc.scalar.copy(c_product[q], hid[0:CR, q]).then_inc(c_out, 1)

            def high_parts(s, i, q):
                sc.wait_ge(c_tr, s + 1)
                need(sc, c_mm, s - 1)
                nc.scalar.copy(c_turned[q][:, 0], acc[:, q, 0:C * CR]).then_inc(c_thi, 1)
                need(sc, c_stored[q], 32 * i)
                for c in range(2):
                    nc.scalar.activation(c_gfull[q][:, c * CR:(c + 1) * CR], acc[:, q, c * CR:(c + 1) * CR],
                                         ACT.Identity, bias=w1c[:, c:c + 1], scale=w3c[:, c:c + 1]
                                         ).then_inc(c_ga, 1)
                if not (isinstance(s, int) and s == 0):
                    product_copy(s - 1, i + q - 1, 1 - q)

            sc.wait_ge(s_chain, 1)
            context_steps(sc, high_parts)

            def g_high(n):
                sc.wait_ge(ctx_in, 128 * (n + 1))
                need(sc, att_done, RT * n)
                nc.scalar.copy(gs[:, 0], g_raw).then_inc(ctx_hi, 1)

            def context_high(n):
                for raw, tail, dst in ((hq_raw, hq_tail, hqs), (hqw_raw, hqw_tail, hqw)):
                    nc.scalar.copy(dst[:, 0], raw).then_inc(ctx_hi, 1)
                    nc.scalar.copy(dst[TAIL:JB, 1], tail[TAIL:JB]).then_inc(ctx_hi, 1)

            def tile_high(b, p, last):
                sc.wait_ge(w_in[p % 2], 16 * (C // 2 + STREAM // 2 * b + p // 2 + 1))
                wait_left(sc, b, p, last)
                nc.scalar.copy(ws[:, (C + p) % 5, 0], w_raw[:, p % 2]).then_inc(w_hi, 1)

            def w1_high(g, f, fresh):
                if not fresh:
                    sc.wait_ge(hid_done, g - 1)
                nc.scalar.copy(w1s[:, f % 2, 0], w1_sb[:, :, f * P:(f + 1) * P]).then_inc(w1_hi, 1)

            def phase_and_hidden(b, f):
                g = FT * b + f
                sc.wait_ge(hid_done, g + 1)
                need(sc, q_done, g - 1)
                nc.scalar.activation(ph[:, f % 2], hid[:, f % 2], ACT.Identity, bias=hbias[:, f:f + 1],
                                     scale=HSCALE).then_inc(t_done, 1)
                need(sc, act_lo, g - 1)
                nc.scalar.activation(h2[:, f % 2], hid[:, f % 2], ACT.Identity, bias=b1c[:, f:f + 1],
                                     scale=1.0).then_inc(h2_done, 1)

            def relu_high(g, f):
                sc.wait_ge(q_done, g + 1)
                need(sc, ffn2_done, g - 3)
                nc.scalar.activation(act[:, f % 4, 0], h2[:, f % 2], ACT.Relu).then_inc(act_hi, 1)

            def sine(b, f):
                sc.wait_ge(r_done, FT * b + f + 1)
                nc.scalar.activation(ph[:, f % 2], ph[:, f % 2], ACT.Sin, scale=TWO_PI_BELOW).then_inc(s_done, 1)

            def sim_bias(n):
                sc.wait_ge(sim_done, n + 1)
                nc.scalar.activation(simt[:], mis[0:J, 0], ACT.Identity, bias=vj[0:J], scale=1.0
                                     ).then_inc(simt_done, 1)

            def exponentials(n):
                sc.wait_ge(shift_done, n + 1)
                nc.scalar.activation(prob[:], prob[:], ACT.Exp).then_inc(exp_done, 1)
                sc.wait_ge(gmax_done, n + 1)
                nc.scalar.activation(e_bc[:], mis[:, 0], ACT.Exp, bias=gmax[:], scale=1.0, accum_out=esum[:]
                                     ).then_inc(ebc_done, 1)

            def prob_high(n):
                sc.wait_ge(prob_done, n + 1)
                nc.scalar.copy(split_high[0], prob[:]).then_inc(split_hi, 1)
                nc.scalar.copy(split_high[1], prob[:]).then_inc(split_hi, 1)

            def stack_out(n):
                sc.wait_ge(at_done, n + 1)
                need(sc, att_done, RT * n)
                nc.scalar.copy(at_s[:, 0], mis[:, 1]).then_inc(at_out, 1)

            def w0_high(n, c):
                sc.wait_ge(w0t_done, C * n + c + 1)
                nc.scalar.copy(w0s[:, c % 2, 0], tmp_w[:]).then_inc(w0_hi, 1)

            def pr_high(n, c):
                sc.wait_ge(prt_done, C * n + c + 1)
                nc.scalar.copy(prs[:, c % 2, 0], full[:, c]).then_inc(pr_hi, 1)

            def attention_first():
                for s in range(CN - LATE, CN - 2):
                    single_step(high_parts, s)
                    if s - (CN - LATE) < 2:
                        turned_high(0, s - (CN - LATE) + 2, 0, tr1, t1_hi)
                g_high(0)
                single_step(high_parts, CN - 2)
                context_high(0)
                sim_bias(0)
                single_step(high_parts, CN - 1)
                exponentials(0)
                prob_high(0)
                single_step(product_copy, CN - 1)
                stack_out(0)
                for c in range(C):
                    w0_high(0, c)
                    pr_high(0, c)
                    if c == 1:
                        sc.wait_ge(s_args, 1)
                        nc.scalar.activation(trig[:], arg[:], ACT.Sin).then_inc(s_trig, 1)
                sc.wait_ge(s_w1, 16)
                w1_high(0, 0, True)
                w1_high(1, 1, True)
                for t in range(RT):
                    turned_high(0, t, 0, tr2, t2_hi)

            def body(b, par, first, last):
                n, pn = b + 1, 1 - par
                for f in range(FT):
                    g = FT * b + f
                    phase_and_hidden(b, f)
                    if f == 7 and not last:
                        prob_high(n)
                    if f < FT - 2 or not last:
                        w1_high(g + 2, (f + 2) % FT, False)
                    if f == NA + 1 and not last:
                        for p in splits(f, last):
                            tile_high(b, p, last)
                    if f > 0 or not first:
                        relu_high(g - 1, (f - 1) % FT)
                    sine(b, f)
                    if last:
                        for p in splits(f, last):
                            tile_high(b, p, last)
                        continue
                    if f == 1:
                        turned_high(n, 0, pn, tr1, t1_hi)
                        turned_high(n, 1, pn, tr1, t1_hi)
                    if f == 3:
                        turned_high(n, 2, pn, tr1, t1_hi)
                        turned_high(n, 3, pn, tr1, t1_hi)
                    if f == 2:
                        g_high(n)
                        context_high(n)
                    if f == 4:
                        sim_bias(n)
                    if f == 6:
                        exponentials(n)
                    if f == 8:
                        stack_out(n)
                    if f == NA - 1:
                        w0_high(n, 0)
                        pr_high(n, 0)
                    if f == NA:
                        for c in range(1, C):
                            tile_high(b, SPLITS[NA][c - 1], False)
                            w0_high(n, c)
                            pr_high(n, c)
                    if f == NA + 3:
                        turned_high(n, 0, pn, tr2, t2_hi)
                        turned_high(n, 1, pn, tr2, t2_hi)
                    if f == NA + 4:
                        turned_high(n, 2, pn, tr2, t2_hi)
                        turned_high(n, 3, pn, tr2, t2_hi)
                    if f not in (NA, NA + 1):
                        for p in splits(f, last):
                            tile_high(b, p, last)

            def rest():
                relu_high(FT * B - 1, FT - 1)

            batches(sc, attention_first, body, rest)

        @block.vector
        def _(ve):
            chain = [0]

            def link(ins):
                chain[0] += 1
                ins.then_inc(s_chain, 1)
                ve.wait_ge(s_chain, chain[0])

            def low(dst, value, high):
                return ve.tensor_tensor(dst, value, high.bitcast(F32), ALU.subtract)

            def stats_first(n, t):
                if isinstance(n, int) and n == 0:
                    ve.wait_ge(x_in, 16)
                    ve.bn_stats(st[:, t], X[:, 0, t]).then_inc(st1, 1)
                else:
                    ve.wait_ge(xin_in[t % 2], 16 * (RT // 2 * (n - 1) + t // 2 + 1))
                    ve.bn_stats(st[:, t], xin[:, t % 2]).then_inc(st1, 1)

            def norm_first(n, t):
                ve.wait_ge(rs1, RT // 2 * n + t // 2 + 1)
                at_start = isinstance(n, int) and n == 0
                if at_start and t >= 2:
                    ve.wait_ge(tr1, t - 1)
                ve.tensor_scalar(xin[:, t % 2], X[:, 0, t] if at_start else xin[:, t % 2], mv[:, t, 1:2],
                                 rstd[:, t:t + 1], ALU.subtract, ALU.mult).then_inc(xn1, 1)

            def turned_low(n, t, par, high_done, done):
                ve.wait_ge(high_done, RT * n + t + 1)
                low(T[:, par, 1, :, t * P:(t + 1) * P], mis[:, t % 2].rearrange("p (c r) -> p c r", c=C),
                    T[:, par, 0, :, t * P:(t + 1) * P]).then_inc(done, 1)

            def phases():
                link(ve.tensor_scalar(kth[:], phase[:], float(TURN), ROUND, ALU.mult, ALU.add))
                link(ve.tensor_scalar(kth[:], kth[:], -ROUND, None, ALU.add))
                for part in (TP1, TP2, TP3):
                    link(ve.scalar_tensor_tensor(out=phase[:], in0=kth[:], scalar=-part, in1=phase[:],
                                                 op0=ALU.mult, op1=ALU.add))
                link(ve.tensor_scalar(arg[:, 0], phase[:], PI_BELOW, -PI_BELOW, ALU.min, ALU.max))
                link(ve.scalar_tensor_tensor(out=arg[:, 1], in0=arg[:, 0], scalar=-1.0, in1=arg[:, 0],
                                             op0=ALU.mult, op1=ALU.max))
                link(ve.tensor_scalar(arg[:, 1], arg[:, 1], -1.0, float(np.pi / 2), ALU.mult, ALU.add))
                ve.tensor_scalar(kth[:], b1c[:], HSCALE, None, ALU.mult).then_inc(s_args, 1)
                ve.wait_ge(s_args, 1)
                link(ve.scalar_tensor_tensor(out=hbias[:], in0=phase[:], scalar=float(TURN), in1=kth[:],
                                             op0=ALU.mult, op1=ALU.add))
                ve.wait_ge(s_trig, 1)
                link(ve.tensor_tensor(camp[:], trig[:, 1], wre[:], ALU.mult))
                link(ve.tensor_tensor(kth[:], trig[:, 0], wim[:], ALU.mult))
                link(ve.tensor_tensor(camp[:], camp[:], kth[:], ALU.add))
                link(ve.scalar_tensor_tensor(out=camp[:], in0=camp[:], scalar=0.1, in1=wim[:],
                                             op0=ALU.mult, op1=ALU.mult))

            for t in range(RT):
                stats_first(0, t)
            norm_first(0, 0)
            norm_first(0, 1)
            for c in range(C):
                ve.wait_ge(s_w1q_hi, c + 1)
                low(w1q[:, 1, c], w1q_raw[:, c], w1q[:, 0, c]).then_inc(s_w1q_lo, 1)
            turned_low(0, 0, 0, t1_hi, t1_lo)
            turned_low(0, 1, 0, t1_hi, t1_lo)
            ve.wait_ge(s_cols, 1)
            link(ve.tensor_copy(cols[:], hid[:, 0, 0:NV]))
            norm_first(0, 2)
            norm_first(0, 3)

            def low_parts(s, i, q):
                ve.wait_ge(c_raw[q], 16 * i + 16)
                need(ve, c_vr, s)
                ve.tensor_tensor_reduce(out=kk[0:CR], in0=c_rows[q], in1=e_bc[0:CR], scale=1.0, scalar=0.0,
                                        op0=ALU.mult, op1=ALU.add, accum_out=vraw[0:CR, q:q + 1]
                                        ).then_inc(c_vr, 1)
                ve.wait_ge(c_ga, 2 * (s + 1))
                low(c_turned[q][:, 1], acc[:, q, 0:C * CR], c_turned[q][:, 0]).then_inc(c_tlo, 1)
                need(ve, c_stored[q], 32 * i)
                ve.wait_ge(c_vr, s + 1)
                ve.tensor_tensor(vsum[0:CR, q:q + 1], vraw[0:CR, q:q + 1], bsim[0:CR], ALU.add).then_inc(c_v, 1)
                for c in range(2, C):
                    ve.tensor_scalar(c_gfull[q][:, c * CR:(c + 1) * CR], acc[:, q, c * CR:(c + 1) * CR],
                                     w3c[:, c:c + 1], w1c[:, c:c + 1], ALU.mult, ALU.add).then_inc(c_gd, 1)

            context_steps(ve, low_parts)

            def sine_term(g, f):
                ve.wait_ge(s_done, g + 1)
                ve.scalar_tensor_tensor(out=h2[:, f % 2], in0=ph[:, f % 2], scalar=camp[:, f:f + 1],
                                        in1=h2[:, f % 2], op0=ALU.mult, op1=ALU.add).then_inc(q_done, 1)

            def reduce_phase(b, f):
                g = FT * b + f
                ve.wait_ge(t_done, g + 1)
                need(ve, r_done, g)
                ve.tensor_scalar(kk[:], ph[:, f % 2], ROUND, -ROUND, ALU.add, ALU.add).then_inc(k_done, 1)
                ve.wait_ge(k_done, g + 1)
                ve.tensor_tensor(ph[:, f % 2], ph[:, f % 2], kk[:], ALU.subtract).then_inc(r_done, 1)

            def relu_low(g, f):
                ve.wait_ge(act_hi, g + 1)
                ve.scalar_tensor_tensor(out=act[:, f % 4, 1], in0=h2[:, f % 2], scalar=0.0,
                                        in1=act[:, f % 4, 0].bitcast(F32), op0=ALU.max, op1=ALU.subtract
                                        ).then_inc(act_lo, 1)

            def g_low(n):
                ve.wait_ge(ctx_hi, 5 * n + 1)
                low(gs[:, 1], g_raw, gs[:, 0]).then_inc(g_lo, 1)

            def row_max(n):
                ve.wait_ge(simr_done, n + 1)
                s = mis[:, 1, 0:RT * J].rearrange("p (t j) -> p t j", t=RT)
                ve.tensor_reduce(rmax[:], s, AX.X, ALU.max).then_inc(rmax_done, 1)
                ve.wait_ge(rmax_done, n + 1)
                ve.tensor_tensor(prob[:], s, rmax[:].unsqueeze(2).to_broadcast([P, RT, J]), ALU.subtract
                                 ).then_inc(shift_done, 1)

            def probabilities(n):
                ve.wait_ge(mbc_done, n + 1)
                ve.tensor_reduce(gmax[:], mis[:, 0], AX.X, ALU.max, negate=True).then_inc(gmax_done, 1)
                ve.wait_ge(exp_done, n + 1)
                ve.tensor_reduce(rsum[:], prob[:], AX.X, ALU.add).then_inc(rsum_done, 1)
                ve.wait_ge(rsum_done, n + 1)
                ve.reciprocal(rrec[:], rsum[:]).then_inc(rrec_done, 1)
                ve.wait_ge(rrec_done, n + 1)
                ve.tensor_tensor(prob[:], prob[:], rrec[:].unsqueeze(2).to_broadcast([P, RT, J]), ALU.mult
                                 ).then_inc(prob_done, 1)
                ve.wait_ge(ebc_done, n + 1)
                ve.reciprocal(erec[:], esum[:]).then_inc(erec_done, 1)

            def prob_low(n):
                ve.wait_ge(split_hi, 2 * n + 2)
                low(split_prob[:, :, J:2 * J], prob[:], split_high[0]).then_inc(split_lo, 1)
                low(split_prob[:, :, 3 * J:2 * J + JB], prob[:, :, JA:J], split_high[0][:, :, JA:J]
                    ).then_inc(split_lo, 1)

            def second_stack_out(n):
                ve.wait_ge(at_done, n + 1)
                ve.tensor_copy(at_s[0:JB, 1], mis[0:JB, 0]).then_inc(at_out, 1)

            def row_mean(n, chunks=range(C)):
                for c in chunks:
                    ve.wait_ge(full_done, C * n + c + 1)
                    need(ve, w0_lo if c == 0 else hbr_done, C * n + c)
                    ve.tensor_tensor_reduce(out=tmp_w[:], in0=full[:, c], in1=e_bc[:], scale=1.0, scalar=0.0,
                                            op0=ALU.mult, op1=ALU.add, accum_out=hb_raw[:, c:c + 1]
                                            ).then_inc(hbr_done, 1)
                if C - 1 not in chunks:
                    return
                ve.wait_ge(hbr_done, C * (n + 1))
                ve.wait_ge(erec_done, n + 1)
                ve.tensor_scalar(hb[:], hb_raw[:], erec[:], None, ALU.mult).then_inc(hb_done, 1)

            def w0_chunk(n, c):
                if c == 0:
                    ve.wait_ge(hb_done, n + 1)
                need(ve, w0_lo, C * n + c)
                ve.scalar_tensor_tensor(out=tmp_w[:], in0=w3_sb[:, c], scalar=hb[:, c:c + 1], in1=w0_sb[:, c],
                                        op0=ALU.mult, op1=ALU.add).then_inc(w0t_done, 1)

            def w0_low(n, c):
                ve.wait_ge(w0_hi, C * n + c + 1)
                low(w0s[:, c % 2, 1], tmp_w[:], w0s[:, c % 2, 0]).then_inc(w0_lo, 1)

            def pr_chunk(n, c):
                ve.wait_ge(hqh_done, C * n + c + 1)
                ve.tensor_tensor(full[:, c], mis[:, c % 2], full[:, c], ALU.mult).then_inc(prt_done, 1)

            def chunk_low(n, c):
                ve.wait_ge(pr_hi, C * n + c + 1)
                low(prs[:, c % 2, 1], full[:, c], prs[:, c % 2, 0]).then_inc(pr_lo, 1)

            def chunk(n, c):
                if c >= 2:
                    ve.wait_ge(chunk_done, (C - 1) * n + c - 1)
                w0_chunk(n, c)
                pr_chunk(n, c)
                w0_low(n, c)
                chunk_low(n, c)

            def evacuate(par, t, done):
                ve.tensor_tensor(X[:, par, t], X[:, par, t], acc[:, t], ALU.add).then_inc(done, 1)

            def attention_and_stats(n, par):
                ve.wait_ge(xb_done, n + 1)
                for t in range(RT):
                    ve.wait_ge(att_done, RT * n + t + 1)
                    evacuate(par, t, x2_done)
                    ve.wait_ge(x2_done, RT * n + t + 1)
                    ve.bn_stats(st[:, t], X[:, par, t]).then_inc(st2, 1)

            def norm_second(n, par, t):
                ve.wait_ge(rs2, t // 2 + 1 if isinstance(n, int) and n == 0 else n + 2)
                if t >= 2:
                    ve.wait_ge(tr2, RT * n + t - 1)
                ve.tensor_scalar(xin[:, t % 2], X[:, par, t], mv[:, t, 1:2], rstd[:, t:t + 1],
                                 ALU.subtract, ALU.mult).then_inc(xn2, 1)

            def add_first_part(b, par):
                ve.wait_ge(xb2_done, 2 * (b + 1))
                ve.wait_ge(ffn2_done, FT * b + NA - LAG)
                for t in range(RT):
                    evacuate(par, t, a_evac)

            def add_last_part(b, par, whole):
                if whole:
                    ve.wait_ge(xb2_done, 2 * (b + 1))
                else:
                    ve.wait_ge(ffn2_done, FT * (b + 1))
                    ve.wait_ge(a_evac, RT * (b + 1))
                for t in range(RT):
                    if whole:
                        ve.wait_ge(last_sum, t + 1)
                    evacuate(par, t, b_evac)

            def attention_first():
                for s in range(CN - LATE, CN - 2):
                    single_step(low_parts, s)
                    if s - (CN - LATE) < 2:
                        turned_low(0, s - (CN - LATE) + 2, 0, t1_hi, t1_lo)
                g_low(0)
                single_step(low_parts, CN - 2)
                single_step(low_parts, CN - 1)
                row_max(0)
                probabilities(0)
                prob_low(0)
                row_mean(0, range(0, C // 2))
                second_stack_out(0)
                row_mean(0, range(C // 2, C))
                ve.wait_ge(s_w03, 32)
                for c in range(C):
                    chunk(0, c)
                    if c == 1:
                        phases()
                attention_and_stats(0, 0)
                for t in range(RT):
                    norm_second(0, 0, t)
                    if t >= 1:
                        turned_low(0, t - 1, 0, t2_hi, t2_lo)
                turned_low(0, RT - 1, 0, t2_hi, t2_lo)

            def body(b, par, first, last):
                n, pn = b + 1, 1 - par
                for f in range(FT):
                    g = FT * b + f
                    if f == NA and not last:
                        add_first_part(b, par)
                    if f == 2 and not last:
                        stats_first(n, 2)
                        stats_first(n, 3)
                    if f == 0 and not last:
                        stats_first(n, 0)
                        stats_first(n, 1)
                    if f == 1 and not last:
                        norm_first(n, 0)
                        norm_first(n, 1)
                    if f == 3 and not last:
                        norm_first(n, 2)
                        norm_first(n, 3)
                    if f == NA + 3 and not last:
                        norm_second(n, pn, 0)
                        norm_second(n, pn, 1)
                    if f == NA + 4 and not last:
                        norm_second(n, pn, 2)
                        norm_second(n, pn, 3)
                    reduce_phase(b, f)
                    if f > 0 or not first:
                        sine_term(g - 1, (f - 1) % FT)
                        if f == 7 and not last:
                            prob_low(n)
                        relu_low(g - 1, (f - 1) % FT)
                    if f == 2 and not first:
                        add_last_part(b - 1, pn, False)
                    if last:
                        continue
                    if f == NA + 1:
                        attention_and_stats(n, pn)
                    if f == 1:
                        turned_low(n, 0, pn, t1_hi, t1_lo)
                        turned_low(n, 1, pn, t1_hi, t1_lo)
                    if f == 2:
                        g_low(n)
                    if f == 3:
                        turned_low(n, 2, pn, t1_hi, t1_lo)
                        turned_low(n, 3, pn, t1_hi, t1_lo)
                    if f == 5:
                        row_max(n)
                    if f == 6:
                        probabilities(n)
                    if f == 7:
                        row_mean(n, range(0, C // 2))
                    if f == NA - 2:
                        second_stack_out(n)
                        row_mean(n, range(C // 2, C))
                    if f == NA - 1:
                        chunk(n, 0)
                    if f == NA:
                        for c in range(1, C):
                            chunk(n, c)
                    if f == NA + 3:
                        turned_low(n, 0, pn, t2_hi, t2_lo)
                        turned_low(n, 1, pn, t2_hi, t2_lo)
                    if f == NA + 4:
                        turned_low(n, 2, pn, t2_hi, t2_lo)
                        turned_low(n, 3, pn, t2_hi, t2_lo)

            def rest():
                g = FT * B - 1
                sine_term(g, FT - 1)
                relu_low(g, FT - 1)
                add_last_part(B - 1, (B - 1) % 2, True)

            batches(ve, attention_first, body, rest)

        @block.gpsimd
        def _(po):
            po.memset(ident[:], 0.0).then_inc(s_ident0, 1)
            po.memset(mhalf[:], -0.5).then_inc(s_mhalf, 1)
            po.memset(eps_t[:], EPS).then_inc(s_mhalf, 1)
            po.memset(quarter[:], 0.25).then_inc(s_mhalf, 1)
            po.memset(ones[:], 1.0).then_inc(s_mhalf, 1)
            po.memset(mscale[:, :, 0:2], 0.5).then_inc(s_mhalf, 1)
            po.memset(mscale[:, :, 2:3], 1.0 / D).then_inc(s_mhalf, 1)
            po.wait_ge(s_ident0, 1)
            po.affine_select(out=ident[:], in_=ident[:], compare_op=ALU.not_equal, fill=1.0, base=0,
                             pattern=[[-1, P]], channel_multiplier=1).then_inc(s_ident, 1)
            po.wait_ge(s_mhalf, 6)

            def w1_low(g, f):
                po.wait_ge(w1_hi, g + 1)
                po.tensor_tensor(w1s[:, f % 2, 1], w1_sb[:, :, f * P:(f + 1) * P], w1s[:, f % 2, 0].bitcast(F32),
                                 ALU.subtract).then_inc(w1_lo, 1)

            def moments(t0, t1, stats_done, stats_count, step, count, done):
                po.wait_ge(stats_done, stats_count)
                halves = st[:, t0:t1].rearrange("p t (h k) -> p t h k", h=2)
                po.tensor_tensor(mv[:, t0:t1], halves[:, :, 0], halves[:, :, 1], ALU.add).then_inc(step, 1)
                po.tensor_tensor(dev[:, t0:t1], halves[:, :, 0, 1], halves[:, :, 1, 1], ALU.subtract).then_inc(step, 1)
                po.wait_ge(step, count - 3)
                po.tensor_tensor(mv[:, t0:t1], mv[:, t0:t1], mscale[:, t0:t1], ALU.mult).then_inc(step, 1)
                po.tensor_tensor(dev[:, t0:t1], dev[:, t0:t1], dev[:, t0:t1], ALU.mult).then_inc(step, 1)
                po.wait_ge(step, count - 1)
                po.tensor_tensor(dev[:, t0:t1], dev[:, t0:t1], quarter[:, t0:t1], ALU.mult).then_inc(step, 1)
                po.wait_ge(step, count)
                po.tensor_tensor(vareps[:, t0:t1], mv[:, t0:t1, 2], dev[:, t0:t1], ALU.add).then_inc(step, 1)
                po.wait_ge(step, count + 1)
                po.tensor_tensor(vareps[:, t0:t1], vareps[:, t0:t1], eps_t[:, t0:t1], ALU.add).then_inc(step, 1)
                po.wait_ge(step, count + 2)
                po.tensor_tensor(rstd[:, t0:t1], vareps[:, t0:t1], mhalf[:, t0:t1], ALU.pow).then_inc(done, 1)

            def deviation_first(n, half):
                moments(2 * half, 2 * half + 2, st1, RT * n + 2 * half + 2, mo1, 7 * (2 * n + half) + 5, rs1)

            def deviation_second(n):
                moments(0, RT, st2, RT * (n + 1), mo2, 7 * (n + 1) + 5, rs2)

            def deviation_second_half(half):
                moments(2 * half, 2 * half + 2, st2, 2 * half + 2, mo2, 7 * half + 5, rs2)

            def whole(n, c, par):
                if c == 0:
                    need(po, pr_lo, C * n)
                    po.wait_ge(t1_lo, RT * (n + 1))
                    po.wait_ge(g_lo, n + 1)
                    po.wait_ge(hq_lo, 2 * (n + 1))
                po.tensor_tensor(full[:, c], T[:, par, 0, c].bitcast(F32), T[:, par, 1, c].bitcast(F32), ALU.add
                                 ).then_inc(full_done, 1)

            def first_tile(c):
                po.wait_ge(w_in[c % 2], 16 * (c // 2 + 1))
                po.tensor_tensor(ws[:, c, 0], w_raw[:, c % 2], ones[:].to_broadcast([P, D]), ALU.mult).then_inc(w_hi, 1)
                po.wait_ge(w_hi, c + 1)
                po.tensor_tensor(ws[:, c, 1], w_raw[:, c % 2], ws[:, c, 0].bitcast(F32), ALU.subtract
                                 ).then_inc(w_lo, 1)

            def tile_low(b, p):
                po.wait_ge(w_hi, count_of(b, p) + 1)
                slot = ws[:, (C + p) % 5]
                po.tensor_tensor(slot[:, 1], w_raw[:, p % 2], slot[:, 0].bitcast(F32), ALU.subtract
                                 ).then_inc(w_lo, 1)

            def context_low(n):
                po.wait_ge(ctx_hi, 5 * (n + 1))
                for raw, dst in ((hq_raw, hqs), (hqw_raw, hqw)):
                    po.tensor_tensor(dst[0:J, 1], raw[0:J], dst[0:J, 0].bitcast(F32), ALU.subtract).then_inc(hq_lo, 1)

            def add_bqv(n, par):
                po.wait_ge(x_in, 16 * (n + 1))
                if isinstance(n, int) and n == 0:
                    po.wait_ge(s_const, 160)
                    po.wait_ge(xn1, RT)
                po.tensor_tensor(X[:, par], X[:, par], bqv_bc[:].unsqueeze(1).to_broadcast([P, RT, D]), ALU.add
                                 ).then_inc(xb_done, 1)

            def add_b2(n, par, t0, t1):
                if t0 == 0:
                    po.wait_ge(xn2, RT * (n + 1))
                po.tensor_tensor(X[:, par, t0:t1], X[:, par, t0:t1],
                                 b2_bc[:].unsqueeze(1).to_broadcast([P, t1 - t0, D]), ALU.add).then_inc(xb2_done, 1)

            deviation_first(0, 0)
            deviation_first(0, 1)
            for c in range(C):
                first_tile(c)
            add_bqv(0, 0)

            def attention_first():
                context_low(0)
                for c in range(C):
                    whole(0, c, 0)
                po.wait_ge(s_w1, 16)
                w1_low(0, 0)
                w1_low(1, 1)
                deviation_second_half(0)
                deviation_second_half(1)
                add_b2(0, 0, 0, 2)

            def body(b, par, first, last):
                n, pn = b + 1, 1 - par
                for f in range(FT):
                    g = FT * b + f
                    if f == 0:
                        if not last:
                            deviation_first(n, 0)
                        add_b2(b, par, 2, RT)
                    if f == 2 and not last:
                        deviation_first(n, 1)
                    if f < FT - 2 or not last:
                        w1_low(g + 2, (f + 2) % FT)
                    for p in splits(f, last):
                        tile_low(b, p)
                    if last:
                        continue
                    if f == 3:
                        context_low(n)
                    if 4 <= f < 4 + C:
                        whole(n, f - 4, pn)
                    if f == NA:
                        add_bqv(n, pn)
                    if f == NA + 1:
                        deviation_second(n)
                    if f == NA + 4:
                        add_b2(n, pn, 0, 2)

            batches(po, attention_first, body, lambda: None)


_INS = ['x', 'ctx_1024', 'L0_xattn_w_sim', 'L0_xattn_b_sim', 'L0_xattn_W_qv', 'L0_xattn_b_qv', 'L0_ffn_W1', 'L0_ffn_b1',
        'L0_ffn_quantum_phases', 'L0_ffn_quantum_weights_real', 'L0_ffn_quantum_weights_imag', 'L0_ffn_W2', 'L0_ffn_b2']


def kernel(**inputs):
    import numpy as _np
    import concourse.bacc as _bacc
    from concourse import mybir as _mybir
    from concourse.bass_utils import run_bass_kernel_spmd as _run

    nc = _bacc.Bacc("TRN2", target_bir_lowering=False, num_devices=1)
    arrays, args = {}, []
    for name in _INS:
        a = _np.ascontiguousarray(inputs[name])
        arrays[f"in_{name}"] = a
        args.append(nc.dram_tensor(f"in_{name}", a.shape, _mybir.dt.from_np(a.dtype), kind="ExternalInput").ap())
    shape = inputs['x'].shape
    args.append(nc.dram_tensor("out_x", shape, _mybir.dt.float32, kind="ExternalOutput").ap())
    xattn_ffn(nc, *args)
    r = _run(nc, [arrays], core_ids=[0])
    return r.results[0]["out_x"]
```
